# Optimizing a Trainium2 kernel written in Bass

```python
import numpy as np
import jax
import jax.numpy as jnp

def _softmax(x, axis=-1):
    return jax.nn.softmax(x, axis=axis)

def _gelu(x):
    return jax.nn.gelu(x, approximate=True)

def _silu(x):
    return jax.nn.silu(x)

def _sigmoid(x):
    return jax.nn.sigmoid(x)

def _layernorm(x, axis=-1, eps=1e-05):
    m = jnp.mean(x, axis=axis, keepdims=True)
    v = jnp.var(x, axis=axis, keepdims=True)
    return (x - m) / jnp.sqrt(v + eps)

def _scatter_add(tgt, idx, src, axis=0):
    return tgt.at[idx].add(src)

def _segment_sum(src, seg, n):
    return jax.ops.segment_sum(src, seg, n)
kernel_name = 'mk_seq_postln_d1_jaxref_r8_6a0ce1'

def setup_inputs(seed: int=0):
    np.random.seed(seed)
    _w = jnp.asarray

    def _L0_attn_setup():
        import math
        import jax, jax.numpy as jnp
        import numpy as np
        NUM_HEAD = 16
        BLOCK_SIZE = 256

        def get_slopes(n):

            def pow2(n):
                start = 2 ** (-2 ** (-(math.log2(n) - 3)))
                return [start * start ** i for i in range(n)]
            if math.log2(n).is_integer():
                return pow2(n)
            c = 2 ** math.floor(math.log2(n))
            return pow2(c) + get_slopes(2 * c)[0::2][:n - c]
        key = jax.random.key(seed)
        ks = jax.random.split(key, 5)
        B, T, C = (4, 256, 128)
        x = jax.random.normal(ks[0], (B, T, C), dtype=jnp.float32)
        Wq = 0.02 * jax.random.normal(ks[1], (C, C), dtype=jnp.float32)
        Wk = 0.02 * jax.random.normal(ks[2], (C, C), dtype=jnp.float32)
        Wv = 0.02 * jax.random.normal(ks[3], (C, C), dtype=jnp.float32)
        Wo = 0.02 * jax.random.normal(ks[4], (C, C), dtype=jnp.float32)
        return {'x': x, 'Wq': Wq, 'Wk': Wk, 'Wv': Wv, 'Wo': Wo}
    _L0_attn_in = _L0_attn_setup()

    def _L0_ffn_setup():
        import jax, jax.numpy as jnp
        import numpy as np
        D_MODEL = 128
        D_FF = 512
        NUM_EXPERTS = 8
        TOP_K = 2
        SEQ = 128
        BATCH = 2
        key = jax.random.key(seed)
        ks = jax.random.split(key, 7)
        s = 0.02
        x = jax.random.normal(ks[0], (SEQ, BATCH, D_MODEL), dtype=jnp.float32)
        gate_w = jax.random.normal(ks[1], (D_MODEL, NUM_EXPERTS), dtype=jnp.float32) * s
        gate_b = jnp.zeros((NUM_EXPERTS,), dtype=jnp.float32)
        W1 = jax.random.normal(ks[2], (NUM_EXPERTS, D_MODEL, D_FF), dtype=jnp.float32) * s
        b1 = jnp.zeros((NUM_EXPERTS, D_FF), dtype=jnp.float32)
        W2 = jax.random.normal(ks[3], (NUM_EXPERTS, D_FF, D_MODEL), dtype=jnp.float32) * s
        b2 = jnp.zeros((NUM_EXPERTS, D_MODEL), dtype=jnp.float32)
        return {'x': x, 'gate_w': gate_w, 'gate_b': gate_b, 'W1': W1, 'b1': b1, 'W2': W2, 'b2': b2}
    _L0_ffn_in = _L0_ffn_setup()
    _d = {'L0_attn_x': _L0_attn_in['x'], 'L0_attn_Wq': _L0_attn_in['Wq'], 'L0_attn_Wk': _L0_attn_in['Wk'], 'L0_attn_Wv': _L0_attn_in['Wv'], 'L0_attn_Wo': _L0_attn_in['Wo'], 'L0_ffn_gate_w': _L0_ffn_in['gate_w'], 'L0_ffn_gate_b': _L0_ffn_in['gate_b'], 'L0_ffn_W1': _L0_ffn_in['W1'], 'L0_ffn_b1': _L0_ffn_in['b1'], 'L0_ffn_W2': _L0_ffn_in['W2'], 'L0_ffn_b2': _L0_ffn_in['b2']}
    _x0 = _d['L0_attn_x']
    _d['L0_attn_x'] = jax.random.normal(jax.random.fold_in(jax.random.key(seed), 1), (1, 2048, 128), dtype=_x0.dtype)
    del _x0
    return _d

def reference(L0_attn_x, L0_attn_Wq, L0_attn_Wk, L0_attn_Wv, L0_attn_Wo, L0_ffn_gate_w, L0_ffn_gate_b, L0_ffn_W1, L0_ffn_b1, L0_ffn_W2, L0_ffn_b2):

    def _L0_attn_ref(x, Wq, Wk, Wv, Wo):
        import math
        import jax, jax.numpy as jnp
        import numpy as np
        NUM_HEAD = 16
        BLOCK_SIZE = 256

        def get_slopes(n):

            def pow2(n):
                start = 2 ** (-2 ** (-(math.log2(n) - 3)))
                return [start * start ** i for i in range(n)]
            if math.log2(n).is_integer():
                return pow2(n)
            c = 2 ** math.floor(math.log2(n))
            return pow2(c) + get_slopes(2 * c)[0::2][:n - c]
        B, T, C = x.shape
        nh, hd = (NUM_HEAD, C // NUM_HEAD)
        q = (x @ Wq).reshape(B, T, nh, hd).transpose(0, 2, 1, 3)
        k = (x @ Wk).reshape(B, T, nh, hd).transpose(0, 2, 1, 3)
        v = (x @ Wv).reshape(B, T, nh, hd).transpose(0, 2, 1, 3)
        attn = jnp.einsum('bhqd,bhkd->bhqk', q, k) / jnp.sqrt(jnp.float32(hd))
        slopes = jnp.asarray(get_slopes(nh), dtype=jnp.float32)
        bias = slopes[:, None] * (jnp.arange(T, dtype=jnp.float32) - (BLOCK_SIZE - 1))
        attn = attn + bias[None, :, None, :]
        causal = jnp.tril(jnp.ones((T, T), dtype=bool))
        masked = jnp.where(causal[None, None], attn.astype(jnp.float32), jnp.finfo(jnp.float32).min)
        probs = jax.nn.softmax(masked, axis=-1)
        out = jnp.einsum('bhqk,bhkd->bhqd', probs, v)
        out = out.transpose(0, 2, 1, 3).reshape(B, T, C)
        return out @ Wo

    def _L0_ffn_ref(x, gate_w, gate_b, W1, b1, W2, b2):
        import jax, jax.numpy as jnp
        import numpy as np
        D_MODEL = 128
        D_FF = 512
        NUM_EXPERTS = 8
        TOP_K = 2
        SEQ = 128
        BATCH = 2
        S, B, D = x.shape
        x_flat = x.reshape(-1, D)
        scores = x_flat @ gate_w + gate_b
        topk_vals, topk_idx = jax.lax.top_k(scores, TOP_K)
        topk_probs = jax.nn.softmax(topk_vals, axis=-1)
        one_hot = jax.nn.one_hot(topk_idx, NUM_EXPERTS, dtype=x.dtype)
        combine = jnp.einsum('tk,tke->te', topk_probs, one_hot)
        h = jax.nn.relu(jnp.einsum('td,edf->etf', x_flat, W1) + b1[:, None, :])
        y = jnp.einsum('etf,efd->etd', h, W2) + b2[:, None, :]
        out = jnp.einsum('te,etd->td', combine, y)
        return out.reshape(S, B, D)
    x = L0_attn_x
    x = _layernorm(x + _L0_attn_ref(x, L0_attn_Wq, L0_attn_Wk, L0_attn_Wv, L0_attn_Wo), axis=-1)
    x = _layernorm(x + _L0_ffn_ref(x, L0_ffn_gate_w, L0_ffn_gate_b, L0_ffn_W1, L0_ffn_b1, L0_ffn_W2, L0_ffn_b2), axis=-1)
    return x

_drawn_inputs = setup_inputs


def setup_inputs(seed=0):
    import zlib

    import numpy as np

    out = dict(_drawn_inputs(seed))
    spreads = {'L0_ffn_gate_b': (0.0, 0.1), 'L0_ffn_b1': (0.0, 0.379), 'L0_ffn_b2': (0.0, 0.1)}
    factors = {'L0_attn_Wq': 8.0, 'L0_attn_Wk': 8.0, 'L0_attn_Wv': 3.374, 'L0_attn_Wo': 3.436}
    for name, (base, spread) in spreads.items():
        noise = np.random.default_rng([zlib.crc32(name.encode()), seed]).standard_normal(out[name].shape)
        drawn = base * np.exp(spread * noise) if base else spread * noise
        out[name] = jnp.asarray(drawn.astype(out[name].dtype))
    for name, factor in factors.items():
        out[name] = (out[name] * factor).astype(out[name].dtype)
    return out
```

```python
import concourse.bass as bass
from concourse import mybir
from contextlib import ExitStack

T, C, NH, HD = 2048, 128, 16, 8
NE, FF = 8, 512
QT = 512
NQT, NB, NC = T // QT, QT // 128, 128
G = 4
NG = NH // G
TERMS = [(0, 0), (0, 1), (1, 0), (1, 1), (0, 2), (2, 0)]
NT_ROWS = len(TERMS) * HD
CR = 16
VW = HD + 1
NEG_ROW = 6
HROWS = 64
MASKED = -1e30
EPS = 1e-5
LEAD = 4
DOWN_LAG = 2
FC = FF // 128

UNITS = [(qt, g) for qt in range(NQT) for g in range(NG)]
KEYS = [NB * (qt + 1) for qt, _ in UNITS]
START = [sum(KEYS[:u]) for u in range(len(UNITS) + 1)]
STEPS = START[-1]
STEP = [(u, kb) for u in range(len(UNITS)) for kb in range(KEYS[u])]
FSTEP = [(tt, e, fc) for tt in range(NQT) for e in range(NE) for fc in range(FC)]
ALL_STEPS = STEPS + len(FSTEP) + DOWN_LAG + 8

CHUNKS = [[(v, b, j, c) for c in range(UNITS[v][0] + 1) for b in range(NB) for j in range(G)] for v in range(len(UNITS))]
CHUNK_NO = {ch: n for n, ch in enumerate(ch for chs in CHUNKS for ch in chs)}
N_CHUNKS = len(CHUNK_NO)


def chunks_at_steps():
    at = {i: [] for i in range(STEPS)}
    for v in range(2, len(UNITS)):
        first, n = START[v - 1] - LEAD, KEYS[v - 1]
        for k, ch in enumerate(CHUNKS[v]):
            at[first + k * n // len(CHUNKS[v])].append(ch)
    return at


CHUNKS_AT = chunks_at_steps()
MAXED_AFTER = {START[v] - LEAD - 1: v for v in range(2, len(UNITS))}


def side_tasks():
    at = {-1: [("XT", 0), ("Q", 0), ("K", 0), ("V", 0), ("NEG", 0), ("XT", 1), ("Q", 1), ("K", 1), ("V", 1)]}
    for i in range(ALL_STEPS):
        at[i] = []
    for v in range(1, len(UNITS)):
        at[START[v] - 3].append(("NEG", v))
    for tt in range(2, NQT):
        for n, kind in enumerate(("XT", "Q", "K", "V")):
            at[START[NG * (tt - 1)] + n].append((kind, tt))
    for u, (qt, g) in enumerate(UNITS):
        s = START[u + 1]
        at[s + 1].append(("HEADS", u))
        if g == NG - 1:
            for n, kind in ((2, "AT"), (3, "WO"), (6, "X1T"), (7, "GATE"), (9, "CT")):
                at[s + n].append((kind, qt))
    for tt in range(NQT):
        at[STEPS + NE * FC * (tt + 1) + DOWN_LAG + 1].append(("YT", tt))
    return at


SIDE = side_tasks()
TASKS = [t for i in range(-1, ALL_STEPS) for t in SIDE[i]]
TASK_NO = {t: n for n, t in enumerate(TASKS)}


def pair_no(i, p):
    return 2 * i + p


def layer_kernel(nc, x, wq, wk, wv, wo, gate_w, gate_b, w1, b1, w2, b2,
                 ident, ident_h, key_rows, query_rows, mask, mask_turned, pick, iota8, power, out):
    f32, bf16, u32 = mybir.dt.float32, mybir.dt.bfloat16, mybir.dt.uint32
    ALU, ACT, AX = mybir.AluOpType, mybir.ActivationFunctionType, mybir.AxisListType

    q_scratch = nc.dram_tensor("q_scratch", (NH, len(TERMS), HD, T), bf16).ap()
    k_scratch = nc.dram_tensor("k_scratch", (NH, len(TERMS), HD, T), bf16).ap()

    ctx = ExitStack()
    with ctx:
        def sb(name, shape, dt=f32):
            return ctx.enter_context(nc.sbuf_tensor(name, shape, dt))

        def sem(name):
            return ctx.enter_context(nc.semaphore(name))

        id_sb, idh_sb = sb("id_sb", [128, 128]), sb("idh_sb", [128, 128], bf16)
        mask_sb, mask_t = sb("mask_sb", [128, QT]), sb("mask_t_sb", [128, 128], bf16)
        pick_sb = sb("pick_sb", [4 * NE, NE, 128], bf16)
        iota_sb, power_sb = sb("iota_sb", [128, NE]), sb("power_sb", [128, NB])
        wq_sb, wk_sb, wv_sb, wo_sb = (sb(n, [C, C]) for n in ("wq_sb", "wk_sb", "wv_sb", "wo_sb"))
        gw_sb, gb_sb = sb("gw_sb", [C, NE]), sb("gb_sb", [128, NE])
        w1_sb = sb("w1_sb", [C, NE, FF])
        b1_sb = sb("b1_sb", [128, NE, FC])
        w2_sb = sb("w2_sb", [128, NE, FC, C])
        b2_sb = sb("b2_sb", [NE, C])
        x_sb = sb("x_sb", [128, T // 128, C])
        xt_sb = sb("xt_sb", [C, QT])
        q32, k32 = sb("q32", [C, QT]), sb("k32", [C, QT])
        q_rest, k_rest = sb("q_rest", [C, QT]), sb("k_rest", [C, QT])
        q_parts, k_parts = sb("q_parts", [C, 3, QT], bf16), sb("k_parts", [C, 3, QT], bf16)
        q_rows = sb("q_rows", [128, NH, 2, QT], bf16)
        k_rows = sb("k_rows", [128, NH // 2, T], bf16)
        v_sb = sb("v_sb", [128, T // 128, NH * VW + 32 - VW])
        v_heads = v_sb[:, :, 0:NH * VW].rearrange("p t (h c) -> p t h c", c=VW)
        chunk_max = sb("chunk_max", [128, 2, NB * G, NQT])
        dump = sb("dump", [128, 2, QT], bf16)
        row_max = sb("row_max", [128, NB * G])
        max_rest = sb("max_rest", [128, NB * G])
        neg_parts = sb("neg_parts", [128, NB, G, 3], bf16)
        neg_rows = sb("neg_rows", [3 * G, 2, QT], bf16)
        weights = sb("weights", [128, 3, G, QT])
        heads_t = sb("heads_t", [128, QT])
        inv_sum = sb("inv_sum", [128, NB, G])
        heads = sb("heads", [128, NB, C])
        attn_t = sb("attn_t", [C, QT])
        pre = sb("pre", [128, NB, C])
        stats, mean_var = sb("stats", [128, NB, 6]), sb("mean_var", [128, NB, 2])
        var_eps, rstd = sb("var_eps", [128, NB]), sb("rstd", [128, NB])
        x1 = sb("x1", [128, T // 128, C])
        x1_t = sb("x1_t", [C, T])
        score = sb("score", [128, NB, NE])
        top = sb("top", [128, NB, 8])
        top_at, top_atf = sb("top_at", [128, NB, 8], u32), sb("top_atf", [128, NB, 8])
        gap, gap_exp = sb("gap", [128, NB]), sb("gap_exp", [128, NB])
        prob = sb("prob", [128, 3, NB])
        second = sb("second", [128, NB, NE])
        comb = sb("comb", [128, NB, 4 * NE])
        comb_rest, comb_part = sb("comb_rest", [128, NB, NE]), sb("comb_part", [128, 3, NB, NE], bf16)
        comb_t, comb_th = sb("comb_t", [4 * NE, T]), sb("comb_th", [4 * NE, T], bf16)
        relu_sb, hid = weights[:, 0, 0:3, :], weights[:, 1, 0:3, :]
        y_t, pre2 = weights[:, 2, 0, :], weights[:, 2, 1, :].rearrange("p (b c) -> p b c", b=NB)
        out_sb = weights[:, 2, 2:4, :].rearrange("p s (b c) -> p s b c", b=NB)

        bank = ctx.enter_context(nc.psum_tensor("bank", [128, 8, 512], f32))
        MAX_BANK, PV_BANK, SIDE_BANK, COMB_BANK, Y_BANK = 4, 6, 7, 3, 5
        side = bank[:, SIDE_BANK, :]

        consts_in, x_in, w_qkv_in = sem("consts_in"), [sem(f"x_in{t}") for t in range(NQT)], sem("w_qkv_in")
        wo_in, w1_in, w2_in = sem("wo_in"), sem("w1_in"), sem("w2_in")
        const_rows_in = [sem(f"const_rows_in{t}") for t in range(NQT)]
        key_rows_in = sem("key_rows_in")
        v_ready, q_zero = sem("v_ready"), sem("q_zero")
        side_full, side_free = sem("side_full"), sem("side_free")
        q_split, k_split = sem("q_split"), sem("k_split")
        scratch_out = sem("scratch_out")
        rows_in = [sem(f"rows_in{t}") for t in range(NQT)]
        scores_full, max_full, chunks_maxed = sem("scores_full"), sem("max_full"), sem("chunks_maxed")
        neg_ready, vec_negs = sem("neg_ready"), sem("vec_negs")
        neg_in = [sem("neg_in0"), sem("neg_in1")]
        exp_done, pv_done, heads_t_done = sem("exp_done"), sem("pv_done"), sem("heads_t_done")
        var_ready, rstd_ready, x1_ready = sem("var_ready"), sem("rstd_ready"), sem("x1_ready")
        gap_ready, gap_exp_ready, comb_ready = sem("gap_ready"), sem("gap_exp_ready"), sem("comb_ready")
        comb_full, up_full, relu_done, hid_ready, down_done = (sem(n) for n in ("comb_full", "up_full", "relu_done", "hid_ready", "down_done"))
        y_full, y_copied = sem("y_full"), sem("y_copied")
        out_ready, out_stored = sem("out_ready"), [sem("out_stored0"), sem("out_stored1")]
        vec_order, pool_order = sem("vec_order"), sem("pool_order")

        block = ctx.enter_context(nc.Block())

        def tok(tt):
            return slice(tt * QT, (tt + 1) * QT)

        @block.sync
        def _(sp):
            def split_to_rows(tt):
                if tt >= 2:
                    sp.wait_ge(pv_done, 2 * START[NG * (tt - 1)])
                for a in range(2):
                    sp.dma_start(q_rows[HROWS * a:HROWS * a + CR, a::2, tt % 2, :], query_rows[:, a::2, :]).then_inc(const_rows_in[tt], 16)
                for name, parts, scratch, done, which in (("k", k_parts, k_scratch, k_split, 1), ("q", q_parts, q_scratch, q_split, 0)):
                    sp.wait_ge(done, tt + 1)
                    for t, term in enumerate(TERMS):
                        sp.dma_start(scratch[:, t, :, tok(tt)], parts[:, term[which], :]).then_inc(scratch_out, 16)
                sp.wait_ge(scratch_out, 2 * len(TERMS) * 16 * (tt + 1))
                for a in range(2):
                    at = slice(HROWS * a + CR, HROWS * (a + 1))
                    sp.dma_start(k_rows[at, :, tok(tt)],
                                 k_scratch[a::2, :, :, tok(tt)].rearrange("h t d c -> (t d) h c")).then_inc(rows_in[tt], 16)
                    sp.dma_start(q_rows[at, a::2, tt % 2, :],
                                 q_scratch[a::2, :, :, tok(tt)].rearrange("h t d c -> (t d) h c")).then_inc(rows_in[tt], 16)

            def negatives(v):
                qt, g = UNITS[v]
                sp.wait_ge(neg_ready, v + 1)
                for j in range(G):
                    r = HROWS * (j % 2) + NEG_ROW
                    sp.dma_start(q_rows[r:r + 3, G * g + j, qt % 2, :], neg_rows[3 * j:3 * j + 3, v % 2, :]).then_inc(neg_in[v % 2], 16)

            xs = x.rearrange("o (b p) c -> p (o b) c", p=128)
            sp.dma_start(x_sb[:, 0:NB, :], xs[:, 0:NB, :]).then_inc(x_in[0], 16)
            sp.dma_start(id_sb[:, :], ident).then_inc(consts_in, 16)
            for dst, src in ((wq_sb, wq), (wk_sb, wk), (wv_sb, wv)):
                sp.dma_start(dst[:, :], src).then_inc(w_qkv_in, 16)
            for dst, src in ((idh_sb, ident_h), (mask_sb, mask), (mask_t, mask_turned), (pick_sb, pick), (iota_sb, iota8), (power_sb, power)):
                sp.dma_start(dst[:], src).then_inc(consts_in, 16)
            for a in range(2):
                for pr in range(NH // 2):
                    sp.dma_start(k_rows[HROWS * a:HROWS * a + CR, pr, :], key_rows).then_inc(key_rows_in, 16)
            split_to_rows(0)
            for tt in range(1, NQT):
                sp.dma_start(x_sb[:, NB * tt:NB * (tt + 1), :], xs[:, NB * tt:NB * (tt + 1), :]).then_inc(x_in[tt], 16)
            sp.dma_start(wo_sb[:, :], wo).then_inc(wo_in, 16)
            sp.dma_start(gw_sb[:, :], gate_w).then_inc(wo_in, 16)
            sp.dma_start(gb_sb[:, :], gate_b.partition_broadcast(128)).then_inc(wo_in, 16)
            negatives(0)
            split_to_rows(1)
            for e in range(NE):
                sp.dma_start(w1_sb[:, e, :], w1[e]).then_inc(w1_in, 16)
            sp.dma_start(b1_sb[:, :, :], b1).then_inc(w1_in, 16)
            for e in range(NE):
                sp.dma_start(w2_sb[:, e, :, :], w2[e].rearrange("(f p) d -> p f d", p=128)).then_inc(w2_in, 16)
            sp.dma_start(b2_sb[:, :], b2).then_inc(w2_in, 16)
            for v in range(1, len(UNITS)):
                negatives(v)
                if v % NG == 0 and v // NG + 1 < NQT:
                    split_to_rows(v // NG + 1)
            outs = out.rearrange("o (b p) c -> p (o b) c", p=128)
            for tt in range(NQT):
                sp.wait_ge(out_ready, tt + 1)
                sp.dma_start(outs[:, NB * tt:NB * (tt + 1), :], out_sb[:, tt % 2, :, :]).then_inc(out_stored[tt % 2], 16)
            for half in range(2):
                sp.wait_ge(out_stored[half], 16 * (NQT // 2))

        @block.tensor
        def _(pe):
            mm = nc.tensor.matmul

            def transposes(src, dst, idn, n=NB):
                for b in range(n):
                    last = nc.tensor.transpose(dst(b), src(b), idn)
                return last

            def chunk(ch):
                v, b, j, c = ch
                qt, g = UNITS[v]
                n, h = CHUNK_NO[ch], G * g + j
                width = QT if c < qt else 128 * (b + 1)
                if n >= 2:
                    pe.wait_ge(chunks_maxed, n - 1)
                mm(bank[:, MAX_BANK + n % 2, 0:width], q_rows[:, h, qt % 2, 128 * b:128 * (b + 1)],
                   k_rows[:, h // 2, c * QT:c * QT + width], start=True, stop=True).then_inc(max_full, 1)

            def scores(i):
                u, kb = STEP[i]
                qt, g = UNITS[u]
                skip, diagonal = 128 * max(0, kb - NB * qt), kb >= NB * qt
                if kb == 0:
                    pe.wait_ge(neg_in[u % 2], 16 * G * (u // 2 + 1))
                for p in range(2):
                    if i >= 1:
                        pe.wait_ge(exp_done, pair_no(i - 1, p) + 1)
                    for j in (2 * p, 2 * p + 1):
                        h = G * g + j
                        last = mm(bank[:, j, skip:QT], k_rows[:, h // 2, 128 * kb:128 * (kb + 1)],
                                  q_rows[:, h, qt % 2, skip:QT], start=True, stop=not diagonal)
                        if diagonal:
                            last = mm(bank[:, j, skip:skip + 128], idh_sb[:, :], mask_t[:, :], start=False, stop=True)
                    last.then_inc(scores_full, 1)

            def weighted(i):
                u, kb = STEP[i]
                qt, g = UNITS[u]
                skip = 128 * max(0, kb - NB * qt)
                if kb == 0 and u:
                    pe.wait_ge(heads_t_done, u)
                if i == 0:
                    pe.wait_ge(v_ready, 1)
                for p in range(2):
                    pe.wait_ge(exp_done, pair_no(i, p) + 1)
                    for j in (2 * p, 2 * p + 1):
                        last = mm(bank[32 * j:32 * (j + 1), PV_BANK, skip:QT], v_sb[:, kb, VW * (G * g + j):VW * (G * g + j) + 32],
                                  weights[:, i % 3, j, skip:QT], start=kb == 0, stop=kb == KEYS[u] - 1)
                    last.then_inc(pv_done, 1)

            def side_task(kind, n):
                no = TASK_NO[kind, n]
                if no:
                    pe.wait_ge(side_free, no)
                if kind == "XT":
                    pe.wait_ge(x_in[n], 16)
                    if n == 0:
                        pe.wait_ge(consts_in, 16 * 7)
                    last = transposes(lambda b: x_sb[:, NB * n + b, :], lambda b: side[:, 128 * b:128 * (b + 1)], id_sb[:, :])
                elif kind in ("Q", "K"):
                    if n == 0:
                        pe.wait_ge(w_qkv_in, 48)
                    last = mm(side, (wq_sb if kind == "Q" else wk_sb)[:, :], xt_sb[:, :], start=True, stop=True)
                elif kind == "V":
                    for b in range(NB):
                        last = mm(side[:, 128 * b:128 * (b + 1)], xt_sb[:, 128 * b:128 * (b + 1)], wv_sb[:, :], start=True, stop=True)
                elif kind == "NEG":
                    pe.wait_ge(vec_negs, n + 1)
                    view = side[0:3 * G, 0:QT // 2].bitcast(bf16)
                    last = transposes(lambda b: neg_parts[:, b, :, :].rearrange("p j t -> p (j t)"),
                                      lambda b: view[:, 128 * b:128 * (b + 1)], idh_sb[:, :])
                elif kind == "HEADS":
                    pe.wait_ge(heads_t_done, n + 1)
                    last = transposes(lambda b: heads_t[:, 128 * b:128 * (b + 1)], lambda b: side[:, 128 * b:128 * (b + 1)], id_sb[:, :])
                elif kind == "AT":
                    last = transposes(lambda b: heads[:, b, :], lambda b: side[:, 128 * b:128 * (b + 1)], id_sb[:, :])
                elif kind == "WO":
                    pe.wait_ge(wo_in, 48)
                    for b in range(NB):
                        last = mm(side[:, 128 * b:128 * (b + 1)], attn_t[:, 128 * b:128 * (b + 1)], wo_sb[:, :], start=True, stop=True)
                elif kind == "X1T":
                    pe.wait_ge(x1_ready, n + 1)
                    last = transposes(lambda b: x1[:, NB * n + b, :], lambda b: side[:, 128 * b:128 * (b + 1)], id_sb[:, :])
                elif kind == "GATE":
                    for b in range(NB):
                        last = mm(side[:, NE * b:NE * (b + 1)], x1_t[:, n * QT + 128 * b:n * QT + 128 * (b + 1)], gw_sb[:, :], start=True, stop=True)
                elif kind == "CT":
                    pe.wait_ge(comb_ready, n + 1)
                    last = transposes(lambda b: comb[:, b, :], lambda b: side[0:4 * NE, 128 * b:128 * (b + 1)], id_sb[:, :])
                elif kind == "YT":
                    pe.wait_ge(y_copied, n + 1)
                    last = transposes(lambda b: y_t[:, 128 * b:128 * (b + 1)], lambda b: side[:, 128 * b:128 * (b + 1)], id_sb[:, :])
                last.then_inc(side_full, 1)

            def up(k):
                tt, e, fc = FSTEP[k]
                if k == 0:
                    pe.wait_ge(w1_in, 16 * (NE + 1))
                    pe.wait_ge(exp_done, 2 * STEPS)
                    pe.wait_ge(chunks_maxed, N_CHUNKS)
                if fc == 0:
                    no = tt * NE + e
                    if no >= 2:
                        pe.wait_ge(hid_ready, FC * (no - 1))
                    if e == 0:
                        pe.wait_ge(side_free, TASK_NO["CT", tt] + 1)
                    mm(bank[:, COMB_BANK + no % 2, :], pick_sb[:, e, :], comb_th[:, tok(tt)], start=True, stop=True).then_inc(comb_full, 1)
                if k >= 3:
                    pe.wait_ge(relu_done, k - 2)
                mm(bank[:, k % 3, :], w1_sb[:, e, 128 * fc:128 * (fc + 1)], x1_t[:, tok(tt)], start=True, stop=True).then_inc(up_full, 1)

            def down(k):
                tt, e, fc = FSTEP[k]
                y = bank[:, Y_BANK + tt % 2, :]
                if e == 0 and fc == 0:
                    if tt == 0:
                        pe.wait_ge(w2_in, 16 * (NE + 1))
                    if tt == 1:
                        pe.wait_ge(heads_t_done, len(UNITS))
                    if tt >= 2:
                        pe.wait_ge(y_copied, tt - 1)
                    mm(y, b2_sb[:, :], comb_t[0:NE, tok(tt)], start=True, stop=False)
                pe.wait_ge(hid_ready, k + 1)
                last = e == NE - 1 and fc == FC - 1
                done = mm(y, w2_sb[:, e, fc, :], hid[:, k % 3, :], start=False, stop=last)
                done.then_inc(y_full if last else down_done, 1)

            for kind in ("XT", "Q", "K", "V"):
                side_task(kind, 0)
            pe.wait_ge(key_rows_in, 16 * NH)
            pe.wait_ge(q_zero, 1)
            pe.wait_ge(const_rows_in[0], 32)
            pe.wait_ge(rows_in[0], 64)
            for ch in CHUNKS[0]:
                chunk(ch)
            for ch in CHUNKS[1][:len(CHUNKS[1]) // 2]:
                chunk(ch)
            side_task("NEG", 0)
            for ch in CHUNKS[1][len(CHUNKS[1]) // 2:]:
                chunk(ch)
            for kind in ("XT", "Q", "K", "V"):
                side_task(kind, 1)
            for i in range(ALL_STEPS):
                if i < STEPS:
                    scores(i)
                    for ch in CHUNKS_AT[i]:
                        if ch == CHUNKS[ch[0]][0] and ch[0] % NG == 0:
                            tt = ch[0] // NG
                            if tt == 1:
                                pe.wait_ge(q_zero, 2)
                            pe.wait_ge(const_rows_in[tt], 32)
                            pe.wait_ge(rows_in[tt], 64)
                        chunk(ch)
                if 1 <= i <= STEPS:
                    weighted(i - 1)
                k = i - STEPS
                if 0 <= k < len(FSTEP):
                    up(k)
                if 0 <= k - DOWN_LAG < len(FSTEP):
                    down(k - DOWN_LAG)
                for task in SIDE[i]:
                    side_task(*task)

        @block.scalar
        def _(act):
            copy, run = ACT.Copy, nc.scalar.activation

            def exps(i):
                u, kb = STEP[i]
                skip = 128 * max(0, kb - NB * UNITS[u][0])
                for p in range(2):
                    act.wait_ge(scores_full, pair_no(i, p) + 1)
                    if i >= 3:
                        act.wait_ge(pv_done, pair_no(i - 3, p) + 1)
                    run(weights[:, i % 3, 2 * p:2 * p + 2, skip:QT], bank[:, 2 * p:2 * p + 2, skip:QT], ACT.Exp).then_inc(exp_done, 1)

            def sums_out(u):
                act.wait_ge(pv_done, 2 * START[u + 1])
                if u:
                    act.wait_ge(side_full, TASK_NO["HEADS", u - 1] + 1)
                run(heads_t[:, :], bank[:, PV_BANK, :], copy).then_inc(heads_t_done, 1)

            def side_task(kind, n):
                if kind not in ("XT", "Q", "K", "AT", "X1T", "CT"):
                    return
                act.wait_ge(side_full, TASK_NO[kind, n] + 1)
                if kind == "XT":
                    run(xt_sb[:, :], side, copy).then_inc(side_free, 1)
                elif kind == "Q":
                    if n:
                        act.wait_ge(q_split, n)
                    run(q32[:, :], side, copy, scale=float(HD) ** -0.5).then_inc(side_free, 1)
                elif kind == "K":
                    if n:
                        act.wait_ge(k_split, n)
                    run(k32[:, :], side, copy).then_inc(side_free, 1)
                elif kind == "AT":
                    run(attn_t[:, :], side, copy).then_inc(side_free, 1)
                elif kind == "X1T":
                    run(x1_t[:, tok(n)], side, copy).then_inc(side_free, 1)
                elif kind == "CT":
                    run(comb_th[:, tok(n)], side[0:4 * NE, :], copy)
                    run(comb_t[:, tok(n)], side[0:4 * NE, :], copy).then_inc(side_free, 1)

            def gap_exps(n):
                act.wait_ge(gap_ready, n + 1)
                run(gap_exp[:, :], gap[:, :], ACT.Exp).then_inc(gap_exp_ready, 1)

            def relus(k):
                tt, e, fc = FSTEP[k]
                act.wait_ge(up_full, k + 1)
                if k >= 3:
                    act.wait_ge(hid_ready, k - 2)
                run(relu_sb[:, k % 3, :], bank[:, k % 3, :], ACT.Relu, bias=b1_sb[:, e, fc:fc + 1]).then_inc(relu_done, 1)

            def y_out(tt):
                act.wait_ge(y_full, tt + 1)
                if tt:
                    act.wait_ge(side_full, TASK_NO["YT", tt - 1] + 1)
                run(y_t, bank[:, Y_BANK + tt % 2, :], copy).then_inc(y_copied, 1)

            for task in SIDE[-1]:
                side_task(*task)
            for i in range(ALL_STEPS):
                if i < STEPS:
                    exps(i)
                if i in START[1:]:
                    sums_out(START.index(i) - 1)
                k = i - STEPS
                if 0 <= k < len(FSTEP):
                    relus(k)
                if k >= DOWN_LAG + NE * FC and (k - DOWN_LAG) % (NE * FC) == 0:
                    y_out((k - DOWN_LAG) // (NE * FC) - 1)
                for task in SIDE[i]:
                    side_task(*task)
                for kind, n in SIDE.get(i - 1, []):
                    if kind == "GATE":
                        gap_exps(n)

        @block.gpsimd
        def _(pool):
            count = [0]

            def link(ins):
                count[0] += 1
                ins.then_inc(pool_order, 1)
                pool.wait_ge(pool_order, count[0])

            def zero_halves(tt):
                pool.wait_ge(k_split, 1)
                link(nc.gpsimd.memset(q_rows[HROWS:128, 0::2, tt, :].bitcast(u32), 0))
                nc.gpsimd.memset(q_rows[0:HROWS, 1::2, tt, :].bitcast(u32), 0).then_inc(q_zero, 1)
                pool.wait_ge(q_zero, 2)

            def split_k(tt):
                pool.wait_ge(side_free, TASK_NO["K", tt] + 1)
                if tt:
                    pool.wait_ge(scratch_out, 2 * len(TERMS) * 16 * tt)
                link(nc.gpsimd.tensor_copy(k_parts[:, 0, :], k32[:, :]))
                link(nc.gpsimd.tensor_tensor(k_rest[:, :], k32[:, :], k_parts[:, 0, :], ALU.subtract))
                link(nc.gpsimd.tensor_copy(k_parts[:, 1, :], k_rest[:, :]))
                nc.gpsimd.tensor_tensor(k_parts[:, 2, :], k_rest[:, :], k_parts[:, 1, :], ALU.subtract).then_inc(k_split, 1)

            def rstds(n):
                pool.wait_ge(var_ready, n + 1)
                nc.gpsimd.tensor_tensor(rstd[:, :], var_eps[:, :], power_sb[:, :], ALU.pow).then_inc(rstd_ready, 1)

            link(nc.gpsimd.memset(v_sb[:, :, :], 0.0))
            nc.gpsimd.memset(v_heads[:, :, :, HD:HD + 1], 1.0).then_inc(v_ready, 1)
            split_k(0)
            zero_halves(1)
            split_k(1)
            pool.wait_ge(consts_in, 16 * 7)
            for i in range(ALL_STEPS):
                for kind, n in SIDE[i]:
                    if kind == "K":
                        split_k(n)
                    if kind == "WO":
                        rstds(n)
                    if kind == "YT":
                        rstds(NQT + n)

        @block.vector
        def _(dve):
            v_ = nc.vector
            count = [0]

            def link(ins):
                count[0] += 1
                ins.then_inc(vec_order, 1)
                dve.wait_ge(vec_order, count[0])

            def maxes(ch):
                v, b, j, c = ch
                qt, g = UNITS[v]
                n = CHUNK_NO[ch]
                dve.wait_ge(max_full, n + 1)
                to = chunk_max[:, v % 2, b * G + j, c:c + 1]
                if c < qt:
                    v_.tensor_reduce(to, bank[:, MAX_BANK + n % 2, :], axis=AX.X, op=ALU.max).then_inc(chunks_maxed, 1)
                else:
                    w = 128 * (b + 1)
                    if n >= 2:
                        dve.wait_ge(chunks_maxed, n - 1)
                    v_.tensor_tensor_reduce(out=dump[:, n % 2, 0:w], in0=bank[:, MAX_BANK + n % 2, 0:w], in1=mask_sb[:, QT - w:QT],
                                            scale=1.0, scalar=MASKED, op0=ALU.add, op1=ALU.max, accum_out=to).then_inc(chunks_maxed, 1)

            def unit_max(v):
                qt, g = UNITS[v]
                dve.wait_ge(chunks_maxed, CHUNK_NO[CHUNKS[v][-1]] + 1)
                if v:
                    dve.wait_ge(side_full, TASK_NO["NEG", v - 1] + 1)
                link(v_.tensor_reduce(row_max[:, :], chunk_max[:, v % 2, :, 0:qt + 1], axis=AX.X, op=ALU.max))
                parts = neg_parts[:, :, :, :].rearrange("p b j t -> p (b j) t")
                link(v_.tensor_scalar(parts[:, :, 0], row_max[:, :], -1.0, None, ALU.mult))
                link(v_.scalar_tensor_tensor(out=max_rest[:, :], in0=row_max[:, :], scalar=-1.0, in1=parts[:, :, 0],
                                             op0=ALU.mult, op1=ALU.subtract))
                link(v_.tensor_copy(parts[:, :, 1], max_rest[:, :]))
                v_.tensor_tensor(parts[:, :, 2], max_rest[:, :], parts[:, :, 1], ALU.subtract).then_inc(vec_negs, 1)

            def ln_stats(src, n):
                for b in range(NB):
                    link(v_.bn_stats(stats[:, b, :], src[:, b, :]))
                    link(v_.bn_aggr(mean_var[:, b, :], stats[:, b, :]))
                v_.tensor_scalar(var_eps[:, :], mean_var[:, :, 1], EPS, None, ALU.add).then_inc(var_ready, 1)

            def ln_apply(src, dst, n, done):
                dve.wait_ge(rstd_ready, n + 1)
                for b in range(NB):
                    last = v_.tensor_scalar(dst[:, b, :], src[:, b, :], mean_var[:, b, 0:1], rstd[:, b:b + 1], ALU.subtract, ALU.mult)
                last.then_inc(done, 1)

            def split_q(tt):
                dve.wait_ge(side_free, TASK_NO["Q", tt] + 1)
                if tt:
                    dve.wait_ge(scratch_out, 2 * len(TERMS) * 16 * tt)
                link(v_.tensor_copy(q_parts[:, 0, :], q32[:, :]))
                link(v_.tensor_tensor(q_rest[:, :], q32[:, :], q_parts[:, 0, :], ALU.subtract))
                link(v_.tensor_copy(q_parts[:, 1, :], q_rest[:, :]))
                v_.tensor_tensor(q_parts[:, 2, :], q_rest[:, :], q_parts[:, 1, :], ALU.subtract).then_inc(q_split, 1)

            def side_task(kind, n):
                if kind == "Q":
                    split_q(n)
                if kind not in ("V", "NEG", "HEADS", "WO", "GATE", "YT"):
                    return
                dve.wait_ge(side_full, TASK_NO[kind, n] + 1)
                if kind == "V":
                    if n == 0:
                        dve.wait_ge(v_ready, 1)
                    v_.tensor_copy(v_heads[:, NB * n:NB * (n + 1), :, 0:HD],
                                   side.rearrange("p (b h d) -> p b h d", b=NB, h=NH)).then_inc(side_free, 1)
                elif kind == "NEG":
                    if n >= 2:
                        dve.wait_ge(neg_in[n % 2], 16 * G * (n // 2))
                    v_.tensor_copy(neg_rows[:, n % 2, :], side[0:3 * G, 0:QT // 2].bitcast(bf16)).then_inc(neg_ready, 1)
                    dve.wait_ge(neg_ready, n + 1)
                    v_.sem_inc(side_free, 1)
                elif kind == "HEADS":
                    qt, g = UNITS[n]
                    sums = side.rearrange("p (b j r) -> p b j r", b=NB, j=G)
                    if n and g == 0:
                        dve.wait_ge(side_full, TASK_NO["AT", qt - 1] + 1)
                    link(v_.reciprocal(inv_sum[:, :, :], sums[:, :, :, HD]))
                    v_.tensor_tensor(heads[:, :, 32 * g:32 * (g + 1)].rearrange("p b (j d) -> p b j d", j=G), sums[:, :, :, 0:HD],
                                     inv_sum[:, :, :].unsqueeze(3).to_broadcast([128, NB, G, HD]), ALU.mult).then_inc(side_free, 1)
                elif kind == "WO":
                    v_.tensor_tensor(pre[:, :, :], side.rearrange("p (b c) -> p b c", b=NB), x_sb[:, NB * n:NB * (n + 1), :],
                                     ALU.add).then_inc(side_free, 1)
                    dve.wait_ge(side_free, TASK_NO[kind, n] + 1)
                    ln_stats(pre, n)
                elif kind == "GATE":
                    v_.tensor_tensor(score[:, :, :], side[:, 0:NB * NE].rearrange("p (b e) -> p b e", b=NB),
                                     gb_sb[:, :].unsqueeze(1).to_broadcast([128, NB, NE]), ALU.add).then_inc(side_free, 1)
                    dve.wait_ge(side_free, TASK_NO[kind, n] + 1)
                    for b in range(NB):
                        link(v_.max(top[:, b, :], score[:, b, :]))
                        link(v_.max_index(top_at[:, b, :], top[:, b, :], score[:, b, :]))
                    v_.tensor_tensor(gap[:, :], top[:, :, 1], top[:, :, 0], ALU.subtract).then_inc(gap_ready, 1)
                    link(v_.tensor_copy(top_atf[:, :, :], top_at[:, :, :]))
                elif kind == "YT":
                    v_.tensor_tensor(pre2, side.rearrange("p (b c) -> p b c", b=NB), x1[:, NB * n:NB * (n + 1), :],
                                     ALU.add).then_inc(side_free, 1)
                    dve.wait_ge(side_free, TASK_NO[kind, n] + 1)
                    ln_stats(pre2, NQT + n)

            def combine(n):
                dve.wait_ge(gap_exp_ready, n + 1)
                if n:
                    dve.wait_ge(side_full, TASK_NO["CT", n - 1] + 1)
                link(v_.tensor_scalar(prob[:, 2, :], gap_exp[:, :], 1.0, None, ALU.add))
                link(v_.reciprocal(prob[:, 0, :], prob[:, 2, :]))
                link(v_.tensor_tensor(prob[:, 1, :], prob[:, 0, :], gap_exp[:, :], ALU.mult))
                for b in range(NB):
                    v_.tensor_scalar(comb[:, b, 0:NE], iota_sb[:, :], top_atf[:, b, 0:1], prob[:, 0, b:b + 1], ALU.is_equal, ALU.mult)
                    last = v_.tensor_scalar(second[:, b, :], iota_sb[:, :], top_atf[:, b, 1:2], prob[:, 1, b:b + 1], ALU.is_equal, ALU.mult)
                link(last)
                link(v_.tensor_tensor(comb[:, :, 0:NE], comb[:, :, 0:NE], second[:, :, :], ALU.add))
                link(v_.tensor_copy(comb_part[:, 0, :, :], comb[:, :, 0:NE]))
                link(v_.tensor_tensor(comb_rest[:, :, :], comb[:, :, 0:NE], comb_part[:, 0, :, :], ALU.subtract))
                link(v_.tensor_copy(comb_part[:, 1, :, :], comb_rest[:, :, :]))
                link(v_.tensor_tensor(comb_part[:, 2, :, :], comb_rest[:, :, :], comb_part[:, 1, :, :], ALU.subtract))
                v_.tensor_copy(comb[:, :, NE:4 * NE].rearrange("p b (t e) -> p b t e", t=3),
                               comb_part[:, :, :, :].rearrange("p t b e -> p b t e")).then_inc(comb_ready, 1)

            def weigh(k):
                tt, e, fc = FSTEP[k]
                no = tt * NE + e
                dve.wait_ge(relu_done, k + 1)
                if fc == 0:
                    dve.wait_ge(comb_full, no + 1)
                if k >= 3:
                    kk = k - 3
                    dve.wait_ge(y_full, (kk + 1) // (NE * FC)) if (kk + 1) % (NE * FC) == 0 else dve.wait_ge(down_done, kk + 1 - (kk + 1) // (NE * FC))
                v_.tensor_tensor(hid[:, k % 3, :], relu_sb[:, k % 3, :], bank[:, COMB_BANK + no % 2, :], ALU.mult).then_inc(hid_ready, 1)

            v_.memset(q_rows[HROWS:128, 0::2, 0, :].bitcast(u32), 0)
            v_.memset(q_rows[0:HROWS, 1::2, 0, :].bitcast(u32), 0).then_inc(q_zero, 1)
            dve.wait_ge(consts_in, 16 * 7)
            for kind in ("Q", "V"):
                side_task(kind, 0)
            for ch in CHUNKS[0]:
                maxes(ch)
            unit_max(0)
            for ch in CHUNKS[1][:len(CHUNKS[1]) // 2]:
                maxes(ch)
            side_task("NEG", 0)
            for ch in CHUNKS[1][len(CHUNKS[1]) // 2:]:
                maxes(ch)
            unit_max(1)
            for kind in ("Q", "V"):
                side_task(kind, 1)
            dve.wait_ge(wo_in, 48)
            for i in range(ALL_STEPS):
                for ch in CHUNKS_AT.get(i, []):
                    maxes(ch)
                if i in MAXED_AFTER:
                    unit_max(MAXED_AFTER[i])
                k = i - STEPS
                if 0 <= k < len(FSTEP):
                    weigh(k)
                for task in SIDE[i]:
                    side_task(*task)
                for kind, n in SIDE.get(i - 2, []):
                    if kind == "WO":
                        ln_apply(pre, x1[:, NB * n:NB * (n + 1), :], n, x1_ready)
                    if kind == "YT":
                        if n >= 2:
                            dve.wait_ge(out_stored[n % 2], 16 * (n // 2))
                        ln_apply(pre2, out_sb[:, n % 2, :, :], NQT + n, out_ready)
                for kind, n in SIDE.get(i - 1, []):
                    if kind == "GATE":
                        combine(n)


def shape_constants():
    import numpy as np
    half = np.dtype("bfloat16")
    start = 2.0 ** (-2.0 ** (3 - NH.bit_length() + 1))
    slopes = np.array([start * start ** h for h in range(NH)], np.float64).astype(np.float32)
    s1 = slopes.astype(half)
    s2 = (slopes - s1.astype(np.float32)).astype(half)
    s3 = (slopes - s1.astype(np.float32) - s2.astype(np.float32)).astype(half)
    parts = np.stack([s1, s2, s3]).astype(np.float32)
    key_rows = np.zeros((CR, T), np.float32)
    key_rows[0:3] = np.arange(T) % 128
    key_rows[3:6] = np.arange(T) // 128
    key_rows[NEG_ROW:NEG_ROW + 3] = 1
    query_rows = np.zeros((CR, NH, QT), np.float32)
    query_rows[0:3] = parts[:, :, None]
    query_rows[3:6] = 128 * parts[:, :, None]
    mask = np.zeros((128, QT), np.float32)
    mask[:, QT - 128:] = np.where(np.arange(128)[None, :] > np.arange(128)[:, None], np.float32(MASKED), np.float32(0))
    pick = np.zeros((4 * NE, NE, 128), np.float32)
    for e in range(NE):
        for t in range(1, 4):
            pick[t * NE + e, e, :] = 1
    return {
        "ident": np.eye(128, dtype=np.float32), "ident_h": np.eye(128).astype(half),
        "key_rows": key_rows.astype(half), "query_rows": query_rows.astype(half), "mask": mask, "mask_turned": mask[:, QT - 128:].T.astype(half), "pick": pick.astype(half),
        "iota8": np.tile(np.arange(NE, dtype=np.float32), (128, 1)), "power": np.full((128, NB), -0.5, np.float32),
    }


_INS = ["L0_attn_x", "L0_attn_Wq", "L0_attn_Wk", "L0_attn_Wv", "L0_attn_Wo", "L0_ffn_gate_w", "L0_ffn_gate_b",
        "L0_ffn_W1", "L0_ffn_b1", "L0_ffn_W2", "L0_ffn_b2"]


def kernel(**inputs):
    import numpy as _np
    import concourse.bacc as _bacc
    from concourse import mybir as _mybir
    from concourse.bass_utils import run_bass_kernel_spmd as _run

    nc = _bacc.Bacc("TRN2", target_bir_lowering=False, num_devices=1)
    arrays, args = {}, []
    given = {name: _np.ascontiguousarray(inputs[name]) for name in _INS}
    b1 = given["L0_ffn_b1"].reshape(NE, FC, 128)
    given["L0_ffn_b1"] = _np.ascontiguousarray(b1.transpose(2, 0, 1))
    for name, a in {**given, **shape_constants()}.items():
        arrays[f"in_{name}"] = a
        args.append(nc.dram_tensor(f"in_{name}", a.shape, _mybir.dt.from_np(a.dtype), kind="ExternalInput").ap())
    args.append(nc.dram_tensor("out_0", (1, T, C), _mybir.dt.float32, kind="ExternalOutput").ap())
    layer_kernel(nc, *args)
    r = _run(nc, [arrays], core_ids=[0])
    return r.results[0]["out_0"]
```

```python
import concourse.bass as bass
from concourse import mybir
from contextlib import ExitStack

T, C, NH, HD = 2048, 128, 16, 8
NE, FF = 8, 512
QT = 512
NQT, NB = T // QT, QT // 128
G = 4
NG = NH // G
TERMS = [(0, 0), (0, 1), (1, 0), (1, 1), (0, 2), (2, 0)]
CR = 16
NEG_ROW = 6
HROWS = CR + len(TERMS) * HD
VW = HD + 1
MASKED = -1e30
EPS = 1e-5
FC = FF // 128
LEAD = 13
PV_LAG = G + 1
NW, NQ = 6, 4

UNITS = [(qt, g) for qt in range(NQT) for g in range(NG)]
KEYS = [NB * (qt + 1) for qt, _ in UNITS]
START = [sum(KEYS[:u]) for u in range(len(UNITS) + 1)]
STEP = [(u, kb) for u in range(len(UNITS)) for kb in range(KEYS[u])]
SLOTS = G * len(STEP)
UNIT_SLOT = [G * s for s in START]

CHUNKS = [[(v, b, j, c) for c in range(UNITS[v][0] + 1) for b in range(NB) for j in range(G)] for v in range(len(UNITS))]
CHUNK_NO = {ch: n for n, ch in enumerate(ch for chs in CHUNKS for ch in chs)}
FSTEPS = NE * FC
ALL_SLOTS = SLOTS + 36 + 2 * FSTEPS + 16


CHUNK_RATE = 1.1


def chunk_slots():
    at, ahead, slot = {n: [] for n in range(ALL_SLOTS)}, [], float(SLOTS)
    for ch in sorted(CHUNK_NO, key=CHUNK_NO.get, reverse=True):
        slot = min(UNIT_SLOT[ch[0]] - LEAD, slot) - 1 / CHUNK_RATE
        if slot < 0 or ch[0] < 2:
            ahead.insert(0, ch)
        else:
            assert slot > UNIT_SLOT[max(0, ch[0] - 2)] - LEAD
            at[int(slot)].insert(0, ch)
    return at, ahead


CHUNKS_AT, CHUNKS_AHEAD = chunk_slots()
CHUNKS_AHEAD = [ch for ch in CHUNKS_AHEAD if ch[0] >= 2]
MAXED_AFTER = {n: ch[0] for n in range(ALL_SLOTS) for ch in CHUNKS_AT[n] if ch == CHUNKS[ch[0]][-1]}
EXPERTS_FROM = [UNIT_SLOT[NG * (tt + 1)] + 40 for tt in range(NQT)]


def expert_slots():
    at = {n: [] for n in range(ALL_SLOTS)}
    last, late = 16, 26
    for tt in range(NQT):
        k0 = FSTEPS * tt
        ops = [("up", k0)] + [o for k in range(k0 + 1, k0 + FSTEPS) for o in (("up", k), ("down", k - 1))] + [("down", k0 + FSTEPS - 1)]
        n = len(ops)
        for r, op in enumerate(ops):
            if tt == NQT - 1:
                slot = SLOTS + 38 + r
            elif tt == NQT - 2 and r >= n - late:
                slot = SLOTS + 4 + (r - n + late)
            elif tt == NQT - 2 and r >= n - late - last:
                slot = UNIT_SLOT[-2] + (r - n + late + last) * (SLOTS - UNIT_SLOT[-2]) // last
            else:
                k = n - late - last if tt == NQT - 2 else n
                end = UNIT_SLOT[-2] if tt == NQT - 2 else EXPERTS_FROM[tt + 1]
                slot = EXPERTS_FROM[tt] + r * (end - EXPERTS_FROM[tt]) // k
            slot = slot // 2 * 2 + 1 if slot < SLOTS else slot
            at[slot].append(op)
    return at


EXPERTS_AT = expert_slots()
EXPERT_SLOT = {op: n for n in range(ALL_SLOTS) for op in EXPERTS_AT[n]}


def side_slots():
    wanted = []
    for v in range(1, len(UNITS)):
        wanted.append((next((n + 3 for n, w in MAXED_AFTER.items() if w == v), 3), ("NEG", v)))
    for tt in range(2, NQT):
        wanted += [(UNIT_SLOT[NG * (tt - 1)] + 2 * n, (kind, tt)) for n, kind in enumerate(("XT", "K", "Q", "V"))]
    for u, (qt, g) in enumerate(UNITS):
        s = UNIT_SLOT[u + 1] + PV_LAG - G + 1
        wanted.append((s + 1, ("HEADS", u)))
        if g == NG - 1:
            wanted += [(s + n, (kind, qt)) for n, kind in ((4, "AT"), (7, "WO"), (17, "X1T"), (20, "GATE"), (28, "CT"))]
    for m in range(NQT * NE):
        wanted.append((EXPERT_SLOT["up", FC * m] - 1, ("COMB", m)))
    for tt in range(NQT):
        wanted.append((EXPERT_SLOT["down", FSTEPS * (tt + 1) - 1] + 3, ("YT", tt)))
    at, used = {n: None for n in range(ALL_SLOTS)}, set()
    for slot, task in sorted(wanted):
        while slot in used:
            slot += 1
        used.add(slot)
        at[slot] = task
    return at


SIDE = side_slots()
AHEAD = [("XT", 0), ("K", 0), ("Q", 0), ("V", 0), ("XT", 1), ("K", 1), ("NEG", 0), ("Q", 1), ("V", 1)]
TASKS = AHEAD + [SIDE[n] for n in range(ALL_SLOTS) if SIDE[n]]
TASK_NO = {t: n for n, t in enumerate(TASKS)}
SLOT_OF = {t: n for n, t in SIDE.items() if t}


LN_NO = {t: i for i, t in enumerate(t for t in TASKS if t[0] in ("WO", "YT"))}


def slot_of(n):
    u, kb = STEP[n // G]
    d = kb - NB * UNITS[u][0]
    return u, kb, n % G, 128 * max(0, d), d >= 0


def layer_kernel(nc, x, wq, wk, wv, wo, gate_w, gate_b, w1, b1, w2, b2,
                 ident, ident_h, key_rows, query_rows, mask, mask_turned, pick, iota8, power, out):
    f32, f32r, bf16, u32 = mybir.dt.float32, mybir.dt.float32r, mybir.dt.bfloat16, mybir.dt.uint32
    ALU, ACT, AX = mybir.AluOpType, mybir.ActivationFunctionType, mybir.AxisListType

    q_scratch = nc.dram_tensor("q_scratch", (NH, len(TERMS), HD, T), bf16).ap()
    k_scratch = nc.dram_tensor("k_scratch", (NH, len(TERMS), HD, T), bf16).ap()

    ctx = ExitStack()
    with ctx:
        def sb(name, shape, dt=f32):
            return ctx.enter_context(nc.sbuf_tensor(name, shape, dt))

        def sem(name):
            return ctx.enter_context(nc.semaphore(name))

        id_sb, idh_sb = sb("id_sb", [128, 128]), sb("idh_sb", [128, 128], bf16)
        mask_sb, mask_t = sb("mask_sb", [128, QT], bf16), sb("mask_t_sb", [128, 128], bf16)
        pick_sb = sb("pick_sb", [3 * NE, NE, 128], bf16)
        iota_sb, power_sb = sb("iota_sb", [128, NE]), sb("power_sb", [128, NB])
        wq_sb, wk_sb, wv_sb, wo_sb = (sb(n, [C, C]) for n in ("wq_sb", "wk_sb", "wv_sb", "wo_sb"))
        gw_sb, gb_sb = sb("gw_sb", [C, NE]), sb("gb_sb", [128, NE])
        w1_raw = sb("w1_raw", [C, 2, FF])
        w1_hi, w1_lo = sb("w1_hi", [C, NE, FF], f32r), sb("w1_lo", [C, NE, FF], f32r)
        b1_sb = sb("b1_sb", [128, NE, FC])
        w2_sb = sb("w2_sb", [128, NE, FC, C])
        b2_sb = sb("b2_sb", [C, NE])
        x_sb = sb("x_sb", [128, T // 128, C])
        xt_sb = sb("xt_sb", [C, QT])
        q32, k32 = sb("q32", [C, QT]), sb("k32", [C, QT])
        q_rest, k_rest = sb("q_rest", [C, QT]), sb("k_rest", [C, QT])
        q_parts, k_parts = sb("q_parts", [C, 3, QT], bf16), sb("k_parts", [C, 3, QT], bf16)
        q_rows = sb("q_rows", [128, NQ, G, QT], bf16)
        k_rows = sb("k_rows", [128, NH // 2, T], bf16)
        v_sb = sb("v_sb", [128, T // 128, NH * VW + 32 - VW])
        v_heads = v_sb[:, :, 0:NH * VW].rearrange("p t (h c) -> p t h c", c=VW)
        chunk_max = sb("chunk_max", [128, 2, NB * G, NQT])
        dump = sb("dump", [128, 2, QT], bf16)
        row_max = sb("row_max", [128, NB * G])
        max_rest = sb("max_rest", [128, NB * G])
        neg_parts = sb("neg_parts", [128, NB, G // 2, 2, 3], bf16)
        neg_rows = sb("neg_rows", [2 * 3, 2, G // 2, QT], bf16)
        weights = sb("weights", [128, NW, QT])
        heads_t = sb("heads_t", [128, QT])
        inv_sum = sb("inv_sum", [128, NB, G])
        heads = sb("heads", [128, NB, C])
        attn_t = sb("attn_t", [C, QT])
        pre = sb("pre", [128, NB, C])
        stats, mean_var = sb("stats", [128, NB, 6]), sb("mean_var", [128, NB, 2])
        var_eps, rstd = sb("var_eps", [128, NB]), sb("rstd", [128, NB])
        x1 = sb("x1", [128, 2, NB, C])
        x1_t = sb("x1_t", [C, QT])
        x1_hi, x1_lo = sb("x1_hi", [C, 2, QT], f32r), sb("x1_lo", [C, 2, QT], f32r)
        score = sb("score", [128, NB, NE])
        top = sb("top", [128, NB, 8])
        top_at, top_atf = sb("top_at", [128, NB, 8], u32), sb("top_atf", [128, NB, 8])
        gap, gap_exp = sb("gap", [128, NB]), sb("gap_exp", [128, NB])
        prob = sb("prob", [128, 3, NB])
        first, second, comb = sb("first", [128, NB, NE]), sb("second", [128, NB, NE]), sb("comb", [128, NB, NE])
        comb_rest, comb_part = sb("comb_rest", [128, NB, NE]), sb("comb_part", [128, NB, 3, NE], bf16)
        comb_th = sb("comb_th", [3 * NE, 2, QT], bf16)
        comb_b = sb("comb_b", [128, 2, QT])
        hid = sb("hid", [128, 3, QT])
        y_part, y_sum = sb("y_part", [C, 2, QT]), sb("y_sum", [C, QT])
        pre2 = sb("pre2", [128, NB, C])
        stats2, mean_var2 = sb("stats2", [128, NB, 6]), sb("mean_var2", [128, NB, 2])
        out_sb = sb("out_sb", [128, 2, NB, C])

        bank = ctx.enter_context(nc.psum_tensor("bank", [128, 8, 512], f32))
        MAX_BANK, PV_BANK, SIDE_BANK, UP_BANK, Y_BANK = 2, 4, 5, 6, 7
        side = bank[:, SIDE_BANK, :]

        ident_in, consts_in, x_in = sem("ident_in"), sem("consts_in"), [sem(f"x_in{t}") for t in range(NQT)]
        wk_in, wq_in, wv_in, wo_in = sem("wk_in"), sem("wq_in"), sem("wv_in"), sem("wo_in")
        w1_in, b1_in, w2_in = [sem("w1_in0"), sem("w1_in1")], sem("b1_in"), sem("w2_in")
        w1_split, w1_raw_used = sem("w1_split"), sem("w1_raw_used")
        key_rows_in = sem("key_rows_in")
        v_ready, q_zero = sem("v_ready"), sem("q_zero")
        side_full, side_free = sem("side_full"), sem("side_free")
        q_split, k_split = sem("q_split"), sem("k_split")
        k_out, q_out = sem("k_out"), sem("q_out")
        k_in = [sem(f"k_in{t}") for t in range(NQT)]
        q_in = [sem(f"q_in{n}") for n in range(NQ)]
        scores_full, max_full, chunks_maxed = sem("scores_full"), sem("max_full"), sem("chunks_maxed")
        maxed, neg_ready = sem("maxed"), sem("neg_ready")
        neg_in = [sem("neg_in0"), sem("neg_in1")]
        exp_done, pv_done, heads_t_done = sem("exp_done"), sem("pv_done"), sem("heads_t_done")
        var_ready, rstd_ready, x1_ready, x1_hi_ready = sem("var_ready"), sem("rstd_ready"), sem("x1_ready"), sem("x1_hi_ready")
        gap_ready, gap_exp_ready, comb_ready = sem("gap_ready"), sem("gap_exp_ready"), sem("comb_ready")
        up_full, hid_ready, down_done, y_weighed, y_added = (sem(n) for n in ("up_full", "hid_ready", "down_done", "y_weighed", "y_added"))
        out_ready, out_stored = sem("out_ready"), [sem("out_stored0"), sem("out_stored1")]
        vec_order, pool_order = sem("vec_order"), sem("pool_order")

        block = ctx.enter_context(nc.Block())

        def tok(tt):
            return slice(tt * QT, (tt + 1) * QT)

        @block.sync
        def _(sp):
            def parts_out(tt):
                for parts, scratch, ready, done, which in ((k_parts, k_scratch, k_split, k_out, 1), (q_parts, q_scratch, q_split, q_out, 0)):
                    sp.wait_ge(ready, tt + 1)
                    for t, term in enumerate(TERMS):
                        sp.dma_start(scratch[:, t, :, tok(tt)], parts[:, term[which], :]).then_inc(done, 16)
                sp.wait_ge(k_out, len(TERMS) * 16 * (tt + 1))
                for a in range(2):
                    sp.dma_start(k_rows[HROWS * a + CR:HROWS * (a + 1), :, tok(tt)],
                                 k_scratch[a::2, :, :, tok(tt)].rearrange("h t d c -> (t d) h c")).then_inc(k_in[tt], 16)

            def query_rows_in(v):
                qt, g = UNITS[v]
                if v >= NQ:
                    sp.wait_ge(pv_done, UNIT_SLOT[v - NQ + 1])
                for a in range(2):
                    sp.dma_start(q_rows[HROWS * a:HROWS * a + CR, v % NQ, a::2, :],
                                 query_rows[:, G * g + a:G * (g + 1):2, :]).then_inc(q_in[v % NQ], 16)
                if g == 0:
                    sp.wait_ge(q_out, len(TERMS) * 16 * (qt + 1))
                for a in range(2):
                    sp.dma_start(q_rows[HROWS * a + CR:HROWS * (a + 1), v % NQ, a::2, :],
                                 q_scratch[G * g + a:G * (g + 1):2, :, :, tok(qt)].rearrange("h t d c -> (t d) h c")).then_inc(q_in[v % NQ], 16)

            def negatives(v):
                sp.wait_ge(neg_ready, v + 1)
                for a in range(2):
                    r = HROWS * a + NEG_ROW
                    sp.dma_start(q_rows[r:r + 3, v % NQ, a::2, :], neg_rows[3 * a:3 * a + 3, v % 2, :, :]).then_inc(neg_in[v % 2], 16)

            def experts_in():
                sp.dma_start(b1_sb[:, :, :], b1).then_inc(b1_in, 16)
                sp.dma_start(b2_sb[:, :], b2).then_inc(b1_in, 16)
                for e in range(NE):
                    sp.dma_start(w2_sb[:, e, :, :], w2[e].rearrange("(f p) d -> p f d", p=128)).then_inc(w2_in, 16)

            def w1_in_raw(e):
                if e >= 2:
                    sp.wait_ge(w1_split, e - 1)
                sp.dma_start(w1_raw[:, e % 2, :], w1[e]).then_inc(w1_in[e % 2], 16)

            xs = x.rearrange("o (b p) c -> p (o b) c", p=128)
            sp.dma_start(x_sb[:, 0:NB, :], xs[:, 0:NB, :]).then_inc(x_in[0], 16)
            sp.dma_start(id_sb[:, :], ident).then_inc(ident_in, 16)
            for dst, src, done in ((wk_sb, wk, wk_in), (wq_sb, wq, wq_in), (wv_sb, wv, wv_in)):
                sp.dma_start(dst[:, :], src).then_inc(done, 16)
            for a in range(2):
                sp.dma_start(k_rows[HROWS * a:HROWS * a + CR, :, :],
                             key_rows.unsqueeze(1).to_broadcast([CR, NH // 2, T])).then_inc(key_rows_in, 16)
            for dst, src in ((idh_sb, ident_h), (mask_sb, mask), (mask_t, mask_turned), (pick_sb, pick), (iota_sb, iota8), (power_sb, power)):
                sp.dma_start(dst[:], src).then_inc(consts_in, 16)
            parts_out(0)
            query_rows_in(0)
            query_rows_in(1)
            for tt in range(1, NQT):
                sp.dma_start(x_sb[:, NB * tt:NB * (tt + 1), :], xs[:, NB * tt:NB * (tt + 1), :]).then_inc(x_in[tt], 16)
            for dst, src in ((wo_sb, wo), (gw_sb, gate_w), (gb_sb, gate_b.partition_broadcast(128))):
                sp.dma_start(dst[:, :], src).then_inc(wo_in, 16)
            negatives(0)
            query_rows_in(2)
            parts_out(1)
            query_rows_in(3)
            negatives(1)
            w1_in_raw(0)
            w1_in_raw(1)
            for v in range(2, len(UNITS)):
                negatives(v)
                if v % NG == 1 and v // NG + 1 < NQT:
                    parts_out(v // NG + 1)
                if v + 2 < len(UNITS):
                    query_rows_in(v + 2)
                if v - 1 < NE // 2:
                    w1_in_raw(2 * (v - 1))
                    w1_in_raw(2 * (v - 1) + 1)
                if v == NE // 2:
                    experts_in()
            outs = out.rearrange("o (b p) c -> p (o b) c", p=128)
            for tt in range(NQT):
                sp.wait_ge(out_ready, tt + 1)
                sp.dma_start(outs[:, NB * tt:NB * (tt + 1), :], out_sb[:, tt % 2, :, :]).then_inc(out_stored[tt % 2], 16)
            for half in range(2):
                sp.wait_ge(out_stored[half], 16 * (NQT // 2))

        @block.tensor
        def _(pe):
            mm = nc.tensor.matmul

            def chunk(ch):
                v, b, j, c = ch
                qt, g = UNITS[v]
                n = CHUNK_NO[ch]
                width = QT if c < qt else 128 * (b + 1)
                if n >= 2:
                    pe.wait_ge(chunks_maxed, n - 1)
                if ch == CHUNKS[v][0]:
                    pe.wait_ge(q_in[v % NQ], 64 * (v // NQ + 1))
                    if g == 0:
                        pe.wait_ge(k_in[qt], 32)
                mm(bank[:, MAX_BANK + n % 2, 0:width], q_rows[:, v % NQ, j, 128 * b:128 * (b + 1)],
                   k_rows[:, (G * g + j) // 2, c * QT:c * QT + width], start=True, stop=True).then_inc(max_full, 1)

            def scores(n):
                u, kb, j, skip, diagonal = slot_of(n)
                h = G * UNITS[u][1] + j
                if kb == 0 and j == 0:
                    pe.wait_ge(neg_in[u % 2], 32 * (u // 2 + 1))
                if n >= 2:
                    pe.wait_ge(exp_done, n - 1)
                last = mm(bank[:, n % 2, skip:QT], k_rows[:, h // 2, 128 * kb:128 * (kb + 1)],
                          q_rows[:, u % NQ, j, skip:QT], start=True, stop=not diagonal)
                if diagonal:
                    last = mm(bank[:, n % 2, skip:skip + 128], idh_sb[:, :], mask_t[:, :], start=False, stop=True)
                last.then_inc(scores_full, 1)

            def weighted(n):
                u, kb, j, skip, _ = slot_of(n)
                h = G * UNITS[u][1] + j
                if kb == 0 and u and j == 0:
                    pe.wait_ge(heads_t_done, u)
                pe.wait_ge(exp_done, n + 1)
                mm(bank[32 * j:32 * (j + 1), PV_BANK, skip:QT], v_sb[:, kb, VW * h:VW * h + 32],
                   weights[:, n % NW, skip:QT], start=kb == 0, stop=kb == KEYS[u] - 1).then_inc(pv_done, 1)

            def turn(src, dst=lambda b: side[:, 128 * b:128 * (b + 1)], idn=id_sb[:, :], n=NB):
                for b in range(n):
                    last = nc.tensor.transpose(dst(b), src(b), idn)
                return last

            def side_task(kind, n):
                no = TASK_NO[kind, n]
                if no:
                    pe.wait_ge(side_free, no)
                if kind == "XT":
                    pe.wait_ge(x_in[n], 16)
                    if n == 0:
                        pe.wait_ge(ident_in, 16)
                    last = turn(lambda b: x_sb[:, NB * n + b, :])
                elif kind == "K":
                    if n == 0:
                        pe.wait_ge(wk_in, 16)
                    last = mm(side, wk_sb[:, :], xt_sb[:, :], start=True, stop=True)
                elif kind == "Q":
                    if n == 0:
                        pe.wait_ge(wq_in, 16)
                    last = mm(side, wq_sb[:, :], xt_sb[:, :], start=True, stop=True)
                elif kind == "V":
                    if n == 0:
                        pe.wait_ge(wv_in, 16)
                    for b in range(NB):
                        last = mm(side[:, 128 * b:128 * (b + 1)], xt_sb[:, 128 * b:128 * (b + 1)], wv_sb[:, :], start=True, stop=True)
                elif kind == "NEG":
                    pe.wait_ge(maxed, n + 1)
                    view = side[0:6, :].bitcast(bf16)
                    last = turn(lambda i: neg_parts[:, i % NB, i // NB, :, :].rearrange("p j t -> p (j t)"),
                                lambda i: view[:, 128 * i:128 * (i + 1)], idh_sb[:, :], NB * G // 2)
                elif kind == "HEADS":
                    pe.wait_ge(heads_t_done, n + 1)
                    last = turn(lambda b: heads_t[:, 128 * b:128 * (b + 1)])
                elif kind == "AT":
                    last = turn(lambda b: heads[:, b, :])
                elif kind == "WO":
                    pe.wait_ge(wo_in, 48)
                    for b in range(NB):
                        last = mm(side[:, 128 * b:128 * (b + 1)], attn_t[:, 128 * b:128 * (b + 1)], wo_sb[:, :], start=True, stop=True)
                elif kind == "X1T":
                    pe.wait_ge(x1_ready, n + 1)
                    last = turn(lambda b: x1[:, n % 2, b, :])
                elif kind == "GATE":
                    for b in range(NB):
                        last = mm(side[:, NE * b:NE * (b + 1)], x1_t[:, 128 * b:128 * (b + 1)], gw_sb[:, :], start=True, stop=True)
                elif kind == "CT":
                    pe.wait_ge(comb_ready, n + 1)
                    view = side[0:3 * NE, 0:QT // 2].bitcast(bf16)
                    last = turn(lambda b: comb_part[:, b, :, :].rearrange("p t e -> p (t e)"),
                                lambda b: view[:, 128 * b:128 * (b + 1)], idh_sb[:, :])
                elif kind == "COMB":
                    last = mm(side, pick_sb[:, n % NE, :], comb_th[:, n // NE % 2, :], start=True, stop=True)
                elif kind == "YT":
                    pe.wait_ge(y_added, (NE - 1) * (n + 1))
                    last = turn(lambda b: y_sum[:, 128 * b:128 * (b + 1)])
                last.then_inc(side_full, 1)

            def up(k):
                tt, e, fc = k // FSTEPS, k // FC % NE, k % FC
                if tt == 0 and fc == 0:
                    pe.wait_ge(w1_split, e + 1)
                if k % FSTEPS == 0:
                    pe.wait_ge(side_free, TASK_NO["X1T", tt] + 1)
                if k:
                    pe.wait_ge(hid_ready, k)
                f = slice(128 * fc, 128 * (fc + 1))
                mm(bank[:, UP_BANK, :], w1_lo[:, e, f], x1_hi[:, tt % 2, :], start=True, stop=False)
                mm(bank[:, UP_BANK, :], w1_hi[:, e, f], x1_lo[:, tt % 2, :], start=False, stop=False)
                mm(bank[:, UP_BANK, :], w1_hi[:, e, f], x1_hi[:, tt % 2, :], start=False, stop=True).then_inc(up_full, 1)

            def down(k):
                e, fc, m = k // FC % NE, k % FC, k // FC
                if k == 0:
                    pe.wait_ge(w2_in, 16 * NE)
                if fc == 0 and m:
                    pe.wait_ge(y_weighed, m)
                pe.wait_ge(hid_ready, k + 1)
                mm(bank[:, Y_BANK, :], w2_sb[:, e, fc, :], hid[:, k % 3, :], start=fc == 0, stop=fc == FC - 1).then_inc(down_done, 1)

            for kind in ("XT", "K", "Q", "V"):
                side_task(kind, 0)
            pe.wait_ge(q_zero, 1)
            pe.wait_ge(key_rows_in, 32)
            pe.wait_ge(consts_in, 16 * 6)
            for ch in CHUNKS[0]:
                chunk(ch)
            for kind in ("XT", "K", "Q", "V"):
                if kind == "Q":
                    side_task("NEG", 0)
                side_task(kind, 1)
            for ch in CHUNKS[1] + CHUNKS_AHEAD:
                chunk(ch)
            pe.wait_ge(v_ready, 1)
            for n in range(ALL_SLOTS):
                if n < SLOTS:
                    scores(n)
                for ch in CHUNKS_AT[n][:1]:
                    chunk(ch)
                if n % G == PV_LAG % G and 0 <= n - PV_LAG < SLOTS:
                    for j in range(G):
                        weighted(n - PV_LAG + j)
                for ch in CHUNKS_AT[n][1:]:
                    chunk(ch)
                for kind, k in EXPERTS_AT[n]:
                    (up if kind == "up" else down)(k)
                if SIDE[n]:
                    side_task(*SIDE[n])

        @block.scalar
        def _(act):
            copy, run = ACT.Copy, nc.scalar.activation

            def exps(n):
                skip = slot_of(n)[3]
                act.wait_ge(scores_full, n + 1)
                if n >= NW:
                    act.wait_ge(pv_done, n - NW + 1)
                run(weights[:, n % NW, skip:QT], bank[:, n % 2, skip:QT], ACT.Exp).then_inc(exp_done, 1)

            def sums_out(u):
                act.wait_ge(pv_done, UNIT_SLOT[u + 1])
                if u:
                    act.wait_ge(side_full, TASK_NO["HEADS", u - 1] + 1)
                run(heads_t[:, :], bank[:, PV_BANK, :], copy).then_inc(heads_t_done, 1)

            def side_task(kind, n):
                if kind not in ("XT", "Q", "K", "AT", "X1T", "CT", "COMB"):
                    return
                act.wait_ge(side_full, TASK_NO[kind, n] + 1)
                if kind == "XT":
                    run(xt_sb[:, :], side, copy).then_inc(side_free, 1)
                elif kind == "Q":
                    if n:
                        act.wait_ge(q_split, n)
                    run(q32[:, :], side, copy, scale=float(HD) ** -0.5).then_inc(side_free, 1)
                elif kind == "K":
                    if n:
                        act.wait_ge(k_split, n)
                    run(k32[:, :], side, copy).then_inc(side_free, 1)
                elif kind == "AT":
                    run(attn_t[:, :], side, copy).then_inc(side_free, 1)
                elif kind == "X1T":
                    run(x1_t[:, :], side, copy)
                    run(x1_hi[:, n % 2, :], side, copy).then_inc(x1_hi_ready, 1)
                elif kind == "CT":
                    run(comb_th[:, n % 2, :], side[0:3 * NE, 0:QT // 2].bitcast(bf16), copy).then_inc(side_free, 1)
                elif kind == "COMB":
                    if n >= 2:
                        act.wait_ge(y_weighed, n - 1)
                    run(comb_b[:, n % 2, :], side, copy).then_inc(side_free, 1)

            def gap_exps(n):
                act.wait_ge(gap_ready, n + 1)
                run(gap_exp[:, :], gap[:, :], ACT.Exp).then_inc(gap_exp_ready, 1)

            def relus(k):
                e, fc = k // FC % NE, k % FC
                act.wait_ge(up_full, k + 1)
                if k == 0:
                    act.wait_ge(b1_in, 32)
                if k >= 3:
                    act.wait_ge(down_done, k - 2)
                run(hid[:, k % 3, :], bank[:, UP_BANK, :], ACT.Relu, bias=b1_sb[:, e, fc:fc + 1]).then_inc(hid_ready, 1)

            for task in AHEAD:
                side_task(*task)
            for n in range(ALL_SLOTS):
                if n < SLOTS:
                    exps(n)
                if n - PV_LAG + G in UNIT_SLOT[1:]:
                    sums_out(UNIT_SLOT.index(n - PV_LAG + G) - 1)
                for kind, k in EXPERTS_AT[n]:
                    if kind == "up":
                        relus(k)
                if SIDE[n]:
                    side_task(*SIDE[n])
                if n >= 3 and SIDE[n - 3] and SIDE[n - 3][0] == "GATE":
                    gap_exps(SIDE[n - 3][1])

        @block.gpsimd
        def _(pool):
            count = [0]

            def link(ins):
                count[0] += 1
                ins.then_inc(pool_order, 1)
                pool.wait_ge(pool_order, count[0])

            def split_k(tt):
                pool.wait_ge(side_free, TASK_NO["K", tt] + 1)
                pool.wait_ge(k_out, len(TERMS) * 16 * tt)
                link(nc.gpsimd.tensor_copy(k_parts[:, 0, :], k32[:, :]))
                link(nc.gpsimd.tensor_tensor(k_rest[:, :], k32[:, :], k_parts[:, 0, :], ALU.subtract))
                link(nc.gpsimd.tensor_copy(k_parts[:, 1, :], k_rest[:, :]))
                nc.gpsimd.tensor_tensor(k_parts[:, 2, :], k_rest[:, :], k_parts[:, 1, :], ALU.subtract).then_inc(k_split, 1)

            def split_w1(e):
                pool.wait_ge(w1_in[e % 2], 16 * (e // 2 + 1))
                link(nc.gpsimd.tensor_copy(w1_hi[:, e, :], w1_raw[:, e % 2, :]))
                nc.gpsimd.tensor_tensor(w1_lo[:, e, :], w1_raw[:, e % 2, :], w1_hi[:, e, :].bitcast(f32), ALU.subtract).then_inc(w1_split, 1)

            def rstds(n):
                pool.wait_ge(var_ready, n + 1)
                nc.gpsimd.tensor_tensor(rstd[:, :], var_eps[:, :], power_sb[:, :], ALU.pow).then_inc(rstd_ready, 1)

            def add_y(m):
                pool.wait_ge(y_weighed, m + 1)
                nc.gpsimd.tensor_tensor(y_sum[:, :], y_sum[:, :], y_part[:, m % 2, :], ALU.add).then_inc(y_added, 1)
                pool.wait_ge(y_added, m + 1 - (m + NE) // NE)

            link(nc.gpsimd.memset(v_sb[:, :, :], 0.0))
            nc.gpsimd.memset(v_heads[:, :, :, HD:HD + 1], 1.0).then_inc(v_ready, 1)
            pool.wait_ge(consts_in, 16 * 6)
            split_k(1)
            for n in range(ALL_SLOTS):
                if n >= 8 and n % 8 == 0 and n // 8 <= NE:
                    split_w1(n // 8 - 1)
                if SIDE[n]:
                    kind, k = SIDE[n]
                    if kind == "K":
                        split_k(k)
                    if kind in ("WO", "YT"):
                        rstds(LN_NO[kind, k])
                for kind, k in EXPERTS_AT[n]:
                    if kind == "down" and k % FC == FC - 1 and k // FC % NE:
                        add_y(k // FC)

        @block.vector
        def _(dve):
            v_ = nc.vector
            count = [0]

            def link(ins):
                count[0] += 1
                ins.then_inc(vec_order, 1)
                dve.wait_ge(vec_order, count[0])

            def maxes(ch):
                v, b, j, c = ch
                n = CHUNK_NO[ch]
                dve.wait_ge(max_full, n + 1)
                to = chunk_max[:, v % 2, b * G + j, c:c + 1]
                if c < UNITS[v][0]:
                    v_.tensor_reduce(to, bank[:, MAX_BANK + n % 2, :], axis=AX.X, op=ALU.max).then_inc(chunks_maxed, 1)
                else:
                    w = 128 * (b + 1)
                    if n >= 2:
                        dve.wait_ge(chunks_maxed, n - 1)
                    v_.tensor_tensor_reduce(out=dump[:, n % 2, 0:w], in0=bank[:, MAX_BANK + n % 2, 0:w], in1=mask_sb[:, QT - w:QT],
                                            scale=1.0, scalar=MASKED, op0=ALU.add, op1=ALU.max, accum_out=to).then_inc(chunks_maxed, 1)

            def unit_max(v):
                qt, g = UNITS[v]
                dve.wait_ge(chunks_maxed, CHUNK_NO[CHUNKS[v][-1]] + 1)
                if v:
                    dve.wait_ge(side_full, TASK_NO["NEG", v - 1] + 1)
                link(v_.tensor_reduce(row_max[:, :], chunk_max[:, v % 2, :, 0:qt + 1], axis=AX.X, op=ALU.max))
                parts = neg_parts[:, :, :, :, :].rearrange("p b i j t -> p (b i j) t")
                link(v_.tensor_scalar(parts[:, :, 0], row_max[:, :], -1.0, None, ALU.mult))
                link(v_.scalar_tensor_tensor(out=max_rest[:, :], in0=row_max[:, :], scalar=-1.0, in1=parts[:, :, 0],
                                             op0=ALU.mult, op1=ALU.subtract))
                link(v_.tensor_copy(parts[:, :, 1], max_rest[:, :]))
                v_.tensor_tensor(parts[:, :, 2], max_rest[:, :], parts[:, :, 1], ALU.subtract).then_inc(maxed, 1)

            def ln_stats(src, stat, mv):
                for b in range(NB):
                    last = v_.bn_stats(stat[:, b, :], src[:, b, :])
                link(last)
                for b in range(NB):
                    last = v_.bn_aggr(mv[:, b, :], stat[:, b, :])
                link(last)
                v_.tensor_scalar(var_eps[:, :], mv[:, :, 1], EPS, None, ALU.add).then_inc(var_ready, 1)

            def ln_apply(src, mv, dst, n, done):
                dve.wait_ge(rstd_ready, n + 1)
                for b in range(NB):
                    last = v_.tensor_scalar(dst[:, b, :], src[:, b, :], mv[:, b, 0:1], rstd[:, b:b + 1], ALU.subtract, ALU.mult)
                last.then_inc(done, 1)

            def split(whole, rest, parts, done):
                link(v_.tensor_copy(parts[:, 0, :], whole[:, :]))
                link(v_.tensor_tensor(rest[:, :], whole[:, :], parts[:, 0, :], ALU.subtract))
                link(v_.tensor_copy(parts[:, 1, :], rest[:, :]))
                v_.tensor_tensor(parts[:, 2, :], rest[:, :], parts[:, 1, :], ALU.subtract).then_inc(done, 1)

            def side_task(kind, n):
                if kind == "Q":
                    dve.wait_ge(side_free, TASK_NO["Q", n] + 1)
                    if n:
                        dve.wait_ge(q_out, len(TERMS) * 16 * n)
                    split(q32, q_rest, q_parts, q_split)
                if kind == "K" and n == 0:
                    dve.wait_ge(side_free, TASK_NO["K", 0] + 1)
                    split(k32, k_rest, k_parts, k_split)
                if kind not in ("V", "NEG", "HEADS", "WO", "X1T", "GATE", "YT"):
                    return
                dve.wait_ge(side_full, TASK_NO[kind, n] + 1)
                if kind == "V":
                    if n == 0:
                        dve.wait_ge(v_ready, 1)
                    v_.tensor_copy(v_heads[:, NB * n:NB * (n + 1), :, 0:HD],
                                   side.rearrange("p (b h d) -> p b h d", b=NB, h=NH)).then_inc(side_free, 1)
                elif kind == "NEG":
                    if n >= 2:
                        dve.wait_ge(neg_in[n % 2], 32 * (n // 2))
                    v_.tensor_copy(neg_rows[:, n % 2, :, :], side[0:6, :].bitcast(bf16).rearrange("p (i c) -> p i c", i=G // 2)).then_inc(neg_ready, 1)
                    dve.wait_ge(neg_ready, n + 1)
                    v_.sem_inc(side_free, 1)
                elif kind == "HEADS":
                    qt, g = UNITS[n]
                    sums = side.rearrange("p (b j r) -> p b j r", b=NB, j=G)
                    link(v_.reciprocal(inv_sum[:, :, :], sums[:, :, :, HD]))
                    v_.tensor_tensor(heads[:, :, 32 * g:32 * (g + 1)].rearrange("p b (j d) -> p b j d", j=G), sums[:, :, :, 0:HD],
                                     inv_sum[:, :, :].unsqueeze(3).to_broadcast([128, NB, G, HD]), ALU.mult).then_inc(side_free, 1)
                elif kind == "WO":
                    v_.tensor_tensor(pre[:, :, :], side.rearrange("p (b c) -> p b c", b=NB), x_sb[:, NB * n:NB * (n + 1), :],
                                     ALU.add).then_inc(side_free, 1)
                    dve.wait_ge(side_free, TASK_NO[kind, n] + 1)
                    ln_stats(pre, stats, mean_var)
                elif kind == "X1T":
                    dve.wait_ge(x1_hi_ready, n + 1)
                    v_.tensor_tensor(x1_lo[:, n % 2, :], side, x1_hi[:, n % 2, :].bitcast(f32), ALU.subtract).then_inc(side_free, 1)
                elif kind == "GATE":
                    v_.tensor_tensor(score[:, :, :], side[:, 0:NB * NE].rearrange("p (b e) -> p b e", b=NB),
                                     gb_sb[:, :].unsqueeze(1).to_broadcast([128, NB, NE]), ALU.add).then_inc(side_free, 1)
                    dve.wait_ge(side_free, TASK_NO[kind, n] + 1)
                    for b in range(NB):
                        last = v_.max(top[:, b, :], score[:, b, :])
                    link(last)
                    v_.tensor_tensor(gap[:, :], top[:, :, 1], top[:, :, 0], ALU.subtract).then_inc(gap_ready, 1)
                    for b in range(NB):
                        last = v_.max_index(top_at[:, b, :], top[:, b, :], score[:, b, :])
                    link(last)
                    link(v_.tensor_copy(top_atf[:, :, :], top_at[:, :, :]))
                elif kind == "YT":
                    v_.tensor_tensor(pre2[:, :, :], side.rearrange("p (b c) -> p b c", b=NB), x1[:, n % 2, :, :],
                                     ALU.add).then_inc(side_free, 1)
                    dve.wait_ge(side_free, TASK_NO[kind, n] + 1)
                    ln_stats(pre2, stats2, mean_var2)

            def combine(n):
                dve.wait_ge(gap_exp_ready, n + 1)
                link(v_.tensor_scalar(prob[:, 2, :], gap_exp[:, :], 1.0, None, ALU.add))
                link(v_.reciprocal(prob[:, 0, :], prob[:, 2, :]))
                link(v_.tensor_tensor(prob[:, 1, :], prob[:, 0, :], gap_exp[:, :], ALU.mult))
                for b in range(NB):
                    v_.tensor_scalar(first[:, b, :], iota_sb[:, :], top_atf[:, b, 0:1], prob[:, 0, b:b + 1], ALU.is_equal, ALU.mult)
                    last = v_.tensor_scalar(second[:, b, :], iota_sb[:, :], top_atf[:, b, 1:2], prob[:, 1, b:b + 1], ALU.is_equal, ALU.mult)
                link(last)
                link(v_.tensor_tensor(comb[:, :, :], first[:, :, :], second[:, :, :], ALU.add))
                link(v_.tensor_copy(comb_part[:, :, 0, :], comb[:, :, :]))
                link(v_.tensor_tensor(comb_rest[:, :, :], comb[:, :, :], comb_part[:, :, 0, :], ALU.subtract))
                link(v_.tensor_copy(comb_part[:, :, 1, :], comb_rest[:, :, :]))
                v_.tensor_tensor(comb_part[:, :, 2, :], comb_rest[:, :, :], comb_part[:, :, 1, :], ALU.subtract).then_inc(comb_ready, 1)

            def weigh_y(m):
                tt, e = m // NE, m % NE
                dve.wait_ge(down_done, FC * (m + 1))
                dve.wait_ge(side_free, TASK_NO["COMB", m] + 1)
                if m == 0:
                    dve.wait_ge(b1_in, 32)
                if e == 0:
                    if tt:
                        dve.wait_ge(side_full, TASK_NO["YT", tt - 1] + 1)
                    to = y_sum[:, :]
                else:
                    if m >= 3:
                        before = m - 2 if (m - 2) % NE else m - 3
                        dve.wait_ge(y_added, before - before // NE)
                    to = y_part[:, m % 2, :]
                v_.scalar_tensor_tensor(out=to, in0=bank[:, Y_BANK, :], scalar=b2_sb[:, e:e + 1], in1=comb_b[:, m % 2, :],
                                        op0=ALU.add, op1=ALU.mult).then_inc(y_weighed, 1)

            v_.memset(q_rows[HROWS:128, :, 0::2, :].bitcast(u32), 0)
            v_.memset(q_rows[0:HROWS, :, 1::2, :].bitcast(u32), 0).then_inc(q_zero, 1)
            for kind in ("K", "Q", "V"):
                side_task(kind, 0)
            dve.wait_ge(consts_in, 16 * 6)
            for ch in CHUNKS[0]:
                maxes(ch)
            unit_max(0)
            side_task("NEG", 0)
            side_task("Q", 1)
            side_task("V", 1)
            for ch in CHUNKS[1]:
                maxes(ch)
            unit_max(1)
            for ch in CHUNKS_AHEAD:
                maxes(ch)
            dve.wait_ge(wo_in, 48)
            for n in range(ALL_SLOTS):
                for ch in CHUNKS_AT[n]:
                    maxes(ch)
                if n in MAXED_AFTER:
                    unit_max(MAXED_AFTER[n])
                for kind, k in EXPERTS_AT[n]:
                    if kind == "down" and k % FC == FC - 1:
                        weigh_y(k // FC)
                if SIDE[n]:
                    side_task(*SIDE[n])
                late = SIDE.get(n - 6)
                if late and late[0] == "WO":
                    ln_apply(pre, mean_var, x1[:, late[1] % 2, :, :], LN_NO[late], x1_ready)
                if late and late[0] == "YT":
                    if late[1] >= 2:
                        dve.wait_ge(out_stored[late[1] % 2], 16 * (late[1] // 2))
                    ln_apply(pre2, mean_var2, out_sb[:, late[1] % 2, :, :], LN_NO[late], out_ready)
                late = SIDE.get(n - 5)
                if late and late[0] == "GATE":
                    combine(late[1])


def shape_constants():
    import numpy as np
    half = np.dtype("bfloat16")
    start = 2.0 ** (-2.0 ** (3 - NH.bit_length() + 1))
    slopes = np.array([start * start ** h for h in range(NH)], np.float64).astype(np.float32)
    s1 = slopes.astype(half)
    s2 = (slopes - s1.astype(np.float32)).astype(half)
    s3 = (slopes - s1.astype(np.float32) - s2.astype(np.float32)).astype(half)
    parts = np.stack([s1, s2, s3]).astype(np.float32)
    key_rows = np.zeros((CR, T), np.float32)
    key_rows[0:3] = np.arange(T) % 128
    key_rows[3:6] = np.arange(T) // 128
    key_rows[NEG_ROW:NEG_ROW + 3] = 1
    query_rows = np.zeros((CR, NH, QT), np.float32)
    query_rows[0:3] = parts[:, :, None]
    query_rows[3:6] = 128 * parts[:, :, None]
    mask = np.zeros((128, QT), np.float32)
    mask[:, QT - 128:] = np.where(np.arange(128)[None, :] > np.arange(128)[:, None], np.float32(MASKED), np.float32(0))
    pick = np.zeros((3 * NE, NE, 128), np.float32)
    for e in range(NE):
        for t in range(3):
            pick[t * NE + e, e, :] = 1
    return {
        "ident": np.eye(128, dtype=np.float32), "ident_h": np.eye(128).astype(half),
        "key_rows": key_rows.astype(half), "query_rows": query_rows.astype(half), "mask": mask.astype(half), "mask_turned": mask[:, QT - 128:].T.astype(half), "pick": pick.astype(half),
        "iota8": np.tile(np.arange(NE, dtype=np.float32), (128, 1)), "power": np.full((128, NB), -0.5, np.float32),
    }


_INS = ["L0_attn_x", "L0_attn_Wq", "L0_attn_Wk", "L0_attn_Wv", "L0_attn_Wo", "L0_ffn_gate_w", "L0_ffn_gate_b",
        "L0_ffn_W1", "L0_ffn_b1", "L0_ffn_W2", "L0_ffn_b2"]


def kernel(**inputs):
    import numpy as _np
    import concourse.bacc as _bacc
    from concourse import mybir as _mybir
    from concourse.bass_utils import run_bass_kernel_spmd as _run

    nc = _bacc.Bacc("TRN2", target_bir_lowering=False, num_devices=1)
    arrays, args = {}, []
    given = {name: _np.ascontiguousarray(inputs[name]) for name in _INS}
    b1 = given["L0_ffn_b1"].reshape(NE, FC, 128)
    given["L0_ffn_b1"] = _np.ascontiguousarray(b1.transpose(2, 0, 1))
    given["L0_ffn_b2"] = _np.ascontiguousarray(given["L0_ffn_b2"].T)
    for name, a in {**given, **shape_constants()}.items():
        arrays[f"in_{name}"] = a
        args.append(nc.dram_tensor(f"in_{name}", a.shape, _mybir.dt.from_np(a.dtype), kind="ExternalInput").ap())
    args.append(nc.dram_tensor("out_0", (1, T, C), _mybir.dt.float32, kind="ExternalOutput").ap())
    layer_kernel(nc, *args)
    r = _run(nc, [arrays], core_ids=[0])
    return r.results[0]["out_0"]
```

```python
import concourse.bass as bass
from concourse import mybir
from contextlib import ExitStack

T, C, NH, HD = 2048, 128, 16, 8
NE, FF = 8, 512
QT = 512
NQT, NB = T // QT, QT // 128
MAX_BANK, PV_BANK, SIDE_BANK, UP_BANK, Y_BANK = 2, 4, 5, 6, 7
G = 4
NG = NH // G
TERMS = [(2, 0), (0, 0), (1, 0), (0, 2), (1, 1), (0, 1)]
CR = 16
NEG_ROW = 6
HROWS = CR + len(TERMS) * HD
VW = HD + 1
MASKED = -1e30
EPS = 1e-5
FC = FF // 128
PASS_COST, MAX_COST, SPARE_COST = 216, 640, 400
LEAD = 11
PV_LAG = G + 1
AHEAD_CHUNKS = 8
NW, NQ = 6, 4

UNITS = [(qt, g) for qt in range(NQT) for g in range(NG)]
KEYS = [NB * (qt + 1) for qt, _ in UNITS]
START = [sum(KEYS[:u]) for u in range(len(UNITS) + 1)]
STEP = [(u, kb) for u in range(len(UNITS)) for kb in range(KEYS[u])]
SLOTS = G * len(STEP)
UNIT_SLOT = [G * s for s in START]

CHUNKS = [[(v, b, j, c) for c in range(UNITS[v][0] + 1) for b in range(NB) for j in range(G)] for v in range(len(UNITS))]
CHUNK_NO = {ch: n for n, ch in enumerate(ch for chs in CHUNKS for ch in chs)}
FSTEPS = NE * FC
ALL_SLOTS = SLOTS + 36 + 2 * FSTEPS + 16


EXPERTS_FROM = [UNIT_SLOT[NG] + 40, UNIT_SLOT[2 * NG] + 125, UNIT_SLOT[3 * NG] + 146]


def expert_slots():
    at = {n: [] for n in range(ALL_SLOTS)}
    last, late = 16, 34
    for tt in range(NQT):
        k0 = FSTEPS * tt
        ops = [("up", k0), ("up", k0 + 1)] + [o for k in range(k0 + 2, k0 + FSTEPS) for o in (("up", k), ("down", k - 2))]
        ops += [("down", k0 + FSTEPS - 2), ("down", k0 + FSTEPS - 1)]
        n = len(ops)
        for r, op in enumerate(ops):
            if tt == NQT - 1:
                slot = SLOTS + 38 + r
            elif tt == NQT - 2 and r >= n - late:
                slot = SLOTS + 4 + (r - n + late)
            elif tt == NQT - 2 and r >= n - late - last:
                slot = UNIT_SLOT[-2] + (r - n + late + last) * (SLOTS - UNIT_SLOT[-2]) // last
            else:
                k = n - late - last if tt == NQT - 2 else n
                end = UNIT_SLOT[-2] if tt == NQT - 2 else EXPERTS_FROM[tt + 1]
                slot = EXPERTS_FROM[tt] + r * (end - EXPERTS_FROM[tt]) // k
            at[slot].append(op)
    return at


def expert_parts(n):
    if n >= SLOTS:
        return [(op, part) for op in EXPERTS_AT[n] for part in range(3)]
    return [(op, 2 - later) for later in range(3) if n + later < SLOTS for op in EXPERTS_AT[n + later]]


EXPERTS_AT = expert_slots()
EXPERT_SLOT = {op: n for n in range(ALL_SLOTS) for op in EXPERTS_AT[n]}


def chunk_slots():
    todo = [ch for chs in CHUNKS[1:] for ch in chs]
    at, ahead, todo = {n: [] for n in range(ALL_SLOTS)}, todo[:AHEAD_CHUNKS], todo[AHEAD_CHUNKS:]
    spare, opens = 0.0, 0
    for n in range(SLOTS):
        spent = PASS_COST * (1.4 + len(expert_parts(n)))
        spent -= sum(MAX_COST for kind, k in EXPERTS_AT[n] if kind == "down" and k % FC == FC - 1)
        spare = min(spare + spent, SPARE_COST)
        while todo:
            v = todo[0][0]
            opens = UNIT_SLOT[v - NQ + 1] + PV_LAG + 7 if v >= NQ else 0
            late = n >= UNIT_SLOT[v] - LEAD - (CHUNK_NO[CHUNKS[v][-1]] + 1 - CHUNK_NO[todo[0]])
            if n < opens or spare <= 0 and not (late and len(at[n]) < 2):
                break
            ch = todo.pop(0)
            share = 1 if ch[3] < UNITS[ch[0]][0] else (ch[1] + 1) / NB
            spare -= (MAX_COST - PASS_COST) * share + (1 - share) * 150
            at[n].append(ch)
    assert not todo
    return at, ahead


CHUNKS_AT, CHUNKS_AHEAD = chunk_slots()
FOUR_FROM = max(n for n in range(SLOTS) if CHUNKS_AT[n]) + 1
TWO_UPS_FROM = min(k for (kind, k), n in EXPERT_SLOT.items() if kind == "up" and n >= SLOTS)
TWO_YS_FROM = min(k for (kind, k), n in EXPERT_SLOT.items() if kind == "down" and k % FC == 0 and n >= SLOTS) // FC
MAXED_AFTER = {n: ch[0] for n in range(ALL_SLOTS) for ch in CHUNKS_AT[n] if ch == CHUNKS[ch[0]][-1]}
def side_slots():
    wanted = []
    for v in range(1, len(UNITS)):
        wanted.append((next((n + 3 for n, w in MAXED_AFTER.items() if w == v), 0), ("NEG", v)))
    for tt in range(2, NQT):
        wanted += [(UNIT_SLOT[NG * (tt - 1)] + 2 * n, (kind, tt)) for n, kind in enumerate(("XT", "K", "Q", "V"))]
    for u, (qt, g) in enumerate(UNITS):
        s = UNIT_SLOT[u + 1] + PV_LAG - G + 1
        wanted.append((s + 1, ("HEADS", u)))
        if g == NG - 1:
            wanted += [(s + n, (kind, qt)) for n, kind in ((4, "AT"), (7, "WO"), (17, "X1T"), (20, "GATE"), (28, "CT"))]
    for m in range(NQT * NE):
        wanted.append((EXPERT_SLOT["up", FC * m] - 1, ("COMB", m)))
    for tt in range(NQT):
        wanted.append((EXPERT_SLOT["down", FSTEPS * (tt + 1) - 1] + 3, ("YT", tt)))
    at, used = {n: None for n in range(ALL_SLOTS)}, set()
    for slot, task in sorted(wanted):
        while slot in used:
            slot += 1
        used.add(slot)
        at[slot] = task
    return at


SIDE = side_slots()
AHEAD = [("XT", 0), ("K", 0), ("Q", 0), ("V", 0), ("XT", 1), ("K", 1), ("Q", 1), ("V", 1), ("NEG", 0)]
TASKS = AHEAD + [SIDE[n] for n in range(ALL_SLOTS) if SIDE[n]]
TASK_NO = {t: n for n, t in enumerate(TASKS)}
SLOT_OF = {t: n for n, t in SIDE.items() if t}


def score_bank(n):
    return n % 4 if n >= FOUR_FROM else n % 2


def up_bank(k):
    return MAX_BANK if k >= TWO_UPS_FROM and (k - TWO_UPS_FROM) % 2 else UP_BANK


def y_bank(m):
    return MAX_BANK + 1 if m >= TWO_YS_FROM and (m - TWO_YS_FROM) % 2 else Y_BANK


HID_BY_VECTOR = [EXPERT_SLOT["up", k] >= FOUR_FROM and k < TWO_UPS_FROM for k in range(NQT * FSTEPS)]


def count(by_vector, k):
    return sum(1 for i in range(k + 1) if by_vector[i] == by_vector[k])


WEIGHTS_UNIT = [1, 2, 3, 4, 5, 6, 6, 7]
SPLIT_SLOT = [8] + [SLOT_OF["NEG", v] + 4 for v in WEIGHTS_UNIT[1:]]
SPLIT_SLOT[6] += 8
STORE_UNIT = [next((v for v in range(2, len(UNITS)) if SLOT_OF["NEG", v] > SLOT_OF["YT", tt] + 6), len(UNITS)) for tt in range(NQT)]
assert all(not 0 <= SLOT_OF["WO", a] - SLOT_OF["YT", b] <= 6 and not 0 <= SLOT_OF["YT", b] - SLOT_OF["WO", a] <= 6
           for a in range(NQT) for b in range(NQT)), "the two layer norms share a buffer"
HI_BY_VECTOR = [EXPERT_SLOT["up", k] >= FOUR_FROM and (k < TWO_UPS_FROM or k % 2 == 1) for k in range(NQT * FSTEPS)]
ORDER = [op for n in range(ALL_SLOTS) for op in EXPERTS_AT[n]]
SPLIT_AT = {n: [] for n in range(ALL_SLOTS)}
for before, after in zip(ORDER, ORDER[1:]):
    if before[0] == "up":
        SPLIT_AT[EXPERT_SLOT[after]].append(before[1])
LO_BY_VECTOR = [EXPERT_SLOT["up", k] >= FOUR_FROM for k in range(NQT * FSTEPS)]

LN_NO = {t: i for i, t in enumerate(t for t in TASKS if t[0] in ("WO", "YT"))}


def slot_of(n):
    u, kb = STEP[n // G]
    d = kb - NB * UNITS[u][0]
    return u, kb, n % G, 128 * max(0, d), d >= 0


def layer_kernel(nc, x, wq, wk, wv, wo, gate_w, gate_b, w1, b1, w2, b2,
                 ident, ident_h, key_rows, query_rows, mask, mask_turned, pick, iota8, power, out):
    f32, f32r, bf16, u32 = mybir.dt.float32, mybir.dt.float32r, mybir.dt.bfloat16, mybir.dt.uint32
    ALU, ACT, AX = mybir.AluOpType, mybir.ActivationFunctionType, mybir.AxisListType

    q_scratch = nc.dram_tensor("q_scratch", (NH, HD, len(TERMS), T), bf16).ap()
    k_scratch = nc.dram_tensor("k_scratch", (NH, HD, len(TERMS), T), bf16).ap()

    ctx = ExitStack()
    with ctx:
        def sb(name, shape, dt=f32):
            return ctx.enter_context(nc.sbuf_tensor(name, shape, dt))

        def sem(name):
            return ctx.enter_context(nc.semaphore(name))

        id_sb, idh_sb = sb("id_sb", [128, 128]), sb("idh_sb", [128, 128], bf16)
        mask_sb, mask_t = sb("mask_sb", [128, QT], bf16), sb("mask_t_sb", [128, 128], bf16)
        iota_sb, power_sb = sb("iota_sb", [128, NE]), sb("power_sb", [128, NB])
        wq_sb, wk_sb, wv_sb, wo_sb = (sb(n, [C, C]) for n in ("wq_sb", "wk_sb", "wv_sb", "wo_sb"))
        gw_sb, gb_sb = sb("gw_sb", [C, NE]), sb("gb_sb", [128, NE])
        w_raw = sb("w_raw", [128, 2, FF])
        w1_hi, w1_lo = sb("w1_hi", [C, NE, FF], f32r), sb("w1_lo", [C, NE, FF], f32r)
        b1_sb = sb("b1_sb", [128, NE, FC])
        w2_hi, w2_lo = sb("w2_hi", [128, NE, FF], f32r), sb("w2_lo", [128, NE, FF], f32r)
        b2_sb = sb("b2_sb", [C, NE])
        x_sb = sb("x_sb", [128, NQT - 1, NB, C])
        xt_sb = sb("xt_sb", [C, QT])
        q32, k32 = sb("q32", [C, QT]), sb("k32", [C, QT])
        q_parts, k_parts = sb("q_parts", [C, 3, QT], bf16), sb("k_parts", [C, 3, QT], bf16)
        q_rows = sb("q_rows", [128, NQ, G, QT], bf16)
        k_rows = sb("k_rows", [128, NH // 2, T], bf16)
        v_sb = sb("v_sb", [128, T // 128, NH * VW + 32 - VW])
        v_heads = v_sb[:, :, 0:NH * VW].rearrange("p t (h c) -> p t h c", c=VW)
        chunk_max = sb("chunk_max", [128, 2, NB * G, NQT])
        row_max = sb("row_max", [128, NB * G])
        max_rest = sb("max_rest", [128, NB * G])
        neg_parts = sb("neg_parts", [128, NB, G // 2, 2, 3], bf16)
        few_rows = sb("few_rows", [64, 2, G // 2, QT], bf16)
        neg_rows = few_rows[0:2 * 3]
        comb_th = few_rows[32:32 + 3 * NE, 0]
        pick_sb = few_rows[32:32 + 3 * NE, 1].rearrange("p a (b c) -> p (a b) c", c=128)
        weights = sb("weights", [128, NW, QT])
        heads_t = sb("heads_t", [128, QT])
        inv_sum = sb("inv_sum", [128, NB, G])
        heads = sb("heads", [128, NB, C])
        attn_t = heads_t
        pre = sb("pre", [128, NB, C])
        stats, mean_var = sb("stats", [128, NB, 6]), sb("mean_var", [128, NB, 2])
        var_eps, rstd = sb("var_eps", [128, NB]), sb("rstd", [128, NB])
        x1 = sb("x1", [128, 2, NB, C])
        x1_t = xt_sb
        x1_hi, x1_lo = sb("x1_hi", [C, 2, QT], f32r), sb("x1_lo", [C, 2, QT], f32r)
        score = sb("score", [128, NB, NE])
        top = sb("top", [128, NB, 8])
        top_at, top_atf = sb("top_at", [128, NB, 8], u32), sb("top_atf", [128, NB, 8])
        gap, gap_exp = sb("gap", [128, NB]), sb("gap_exp", [128, NB])
        prob = sb("prob", [128, 3, NB])
        first, second, comb = sb("first", [128, NB, NE]), sb("second", [128, NB, NE]), sb("comb", [128, NB, NE])
        comb_rest, comb_part = sb("comb_rest", [128, NB, NE]), sb("comb_part", [128, NB, 3, NE], bf16)
        comb_b = sb("comb_b", [128, 2, QT])
        hid = sb("hid", [128, 2, QT])
        hid_hi, hid_lo = sb("hid_hi", [128, 2, QT], f32r), sb("hid_lo", [128, 2, QT], f32r)
        y_part, y_sum = sb("y_part", [C, 2, QT]), sb("y_sum", [C, QT])
        out_sb = k32[:, :].rearrange("p (b c) -> p b c", b=NB)

        bank = ctx.enter_context(nc.psum_tensor("bank", [128, 8, 512], f32))
        side = bank[:, SIDE_BANK, :]

        ident_in, consts_in, x_in = sem("ident_in"), sem("consts_in"), [sem(f"x_in{t}") for t in range(NQT)]
        wk_in, wq_in, wv_in, wo_in = sem("wk_in"), sem("wq_in"), sem("wv_in"), sem("wo_in")
        w_in, b1_in = [sem("w_in0"), sem("w_in1")], sem("b1_in")
        w_split = sem("w_split")
        key_rows_in = sem("key_rows_in")
        v_ready, q_zero = sem("v_ready"), sem("q_zero")
        side_full, side_free = sem("side_full"), sem("side_free")
        q_split, k_split = sem("q_split"), sem("k_split")
        k_out, q_out = sem("k_out"), sem("q_out")
        k_in = [sem(f"k_in{t}") for t in range(NQT)]
        q_in = [sem(f"q_in{n}") for n in range(NQ)]
        scores_full, max_full, chunks_maxed = sem("scores_full"), sem("max_full"), sem("chunks_maxed")
        maxed, neg_ready = sem("maxed"), sem("neg_ready")
        neg_in = [sem("neg_in0"), sem("neg_in1")]
        exp_done, pv_done, heads_t_done = sem("exp_done"), sem("pv_done"), sem("heads_t_done")
        var_ready, rstd_ready, x1_ready, x1_hi_ready = sem("var_ready"), sem("rstd_ready"), sem("x1_ready"), sem("x1_hi_ready")
        gap_ready, gap_exp_ready, comb_ready = sem("gap_ready"), sem("gap_exp_ready"), sem("comb_ready")
        hid_ready_v, hi_ready, hi_ready_v, lo_ready, lo_ready_v = (sem(n) for n in ("hid_ready_v", "hi_ready", "hi_ready_v", "lo_ready", "lo_ready_v"))
        up_full, hid_ready, down_done, y_weighed, y_added = (sem(n) for n in ("up_full", "hid_ready", "down_done", "y_weighed", "y_added"))
        out_ready, out_stored = sem("out_ready"), sem("out_stored")
        vec_order, pool_order = sem("vec_order"), sem("pool_order")

        block = ctx.enter_context(nc.Block())

        def hid_wait(engine, k):
            engine.wait_ge(hid_ready_v if HID_BY_VECTOR[k] else hid_ready, count(HID_BY_VECTOR, k))

        def hi_wait(engine, k):
            engine.wait_ge(hi_ready_v if HI_BY_VECTOR[k] else hi_ready, count(HI_BY_VECTOR, k))

        def lo_wait(engine, k):
            engine.wait_ge(lo_ready_v if LO_BY_VECTOR[k] else lo_ready, count(LO_BY_VECTOR, k))

        def tok(tt):
            return slice(tt * QT, (tt + 1) * QT)

        @block.sync
        def _(sp):
            def parts_out(tt):
                for parts, scratch, ready, done, which in ((k_parts, k_scratch, k_split, k_out, 1), (q_parts, q_scratch, q_split, q_out, 0)):
                    sp.wait_ge(ready, tt + 1)
                    for part in range(3):
                        at = [t for t, term in enumerate(TERMS) if term[which] == part]
                        every = slice(at[0], at[-1] + 1, at[1] - at[0] if len(at) > 1 else 1)
                        sp.dma_start(scratch[:, :, every, tok(tt)].rearrange("h d t c -> (h d) t c"),
                                     parts[:, part, :].unsqueeze(1).to_broadcast([C, len(at), QT])).then_inc(done, 16)
                sp.wait_ge(k_out, 3 * 16 * (tt + 1))
                for a in range(2):
                    sp.dma_start(k_rows[HROWS * a + CR:HROWS * (a + 1), :, tok(tt)],
                                 k_scratch[a::2, :, :, tok(tt)].rearrange("h d t c -> (d t) h c")).then_inc(k_in[tt], 16)

            def slope_rows_in(v):
                qt, g = UNITS[v]
                if v >= NQ:
                    sp.wait_ge(pv_done, UNIT_SLOT[v - NQ + 1])
                for a in range(2):
                    sp.dma_start(q_rows[HROWS * a:HROWS * a + CR, v % NQ, a::2, :],
                                 query_rows[:, G * g + a:G * (g + 1):2, :]).then_inc(q_in[v % NQ], 16)

            def query_rows_in(v):
                qt, g = UNITS[v]
                if g == 0:
                    sp.wait_ge(q_out, 3 * 16 * (qt + 1))
                for a in range(2):
                    sp.dma_start(q_rows[HROWS * a + CR:HROWS * (a + 1), v % NQ, a::2, :],
                                 q_scratch[G * g + a:G * (g + 1):2, :, :, tok(qt)].rearrange("h d t c -> (d t) h c")).then_inc(q_in[v % NQ], 16)

            def negatives(v):
                sp.wait_ge(neg_ready, v + 1)
                for a in range(2):
                    r = HROWS * a + NEG_ROW
                    sp.dma_start(q_rows[r:r + 3, v % NQ, a::2, :], neg_rows[3 * a:3 * a + 3, v % 2, :, :]).then_inc(neg_in[v % 2], 16)

            def store(tt):
                sp.wait_ge(out_ready, tt + 1)
                sp.dma_start(out.rearrange("o (b p) c -> p (o b) c", p=128)[:, NB * tt:NB * (tt + 1), :], out_sb).then_inc(out_stored, 16)

            def experts_in():
                sp.dma_start(b1_sb[:, :, :], b1).then_inc(b1_in, 16)
                sp.dma_start(b2_sb[:, :], b2).then_inc(b1_in, 16)

            def weights_in(e):
                if e:
                    sp.wait_ge(w_split, 2 * e - 1)
                sp.dma_start(w_raw[:, 0, :], w1[e]).then_inc(w_in[0], 16)
                if e:
                    sp.wait_ge(w_split, 2 * e)
                sp.dma_start(w_raw[:, 1, :].rearrange("p (f d) -> p f d", d=C), w2[e].rearrange("(f p) d -> p f d", p=128)).then_inc(w_in[1], 16)

            xs = x.rearrange("o (b p) c -> p (o b) c", p=128)

            def x_tile_in(tt):
                sp.dma_start(x_sb[:, tt % (NQT - 1), :, :], xs[:, NB * tt:NB * (tt + 1), :]).then_inc(x_in[tt], 16)

            x_tile_in(0)
            sp.dma_start(id_sb[:, :], ident).then_inc(ident_in, 16)
            for dst, src, done in ((wk_sb, wk, wk_in), (wq_sb, wq, wq_in), (wv_sb, wv, wv_in)):
                sp.dma_start(dst[:, :], src).then_inc(done, 16)
            x_tile_in(1)
            for a in range(2):
                sp.dma_start(k_rows[HROWS * a:HROWS * a + CR, :, :],
                             key_rows.unsqueeze(1).to_broadcast([CR, NH // 2, T])).then_inc(key_rows_in, 16)
            for dst, src in ((idh_sb, ident_h), (mask_sb, mask), (mask_t, mask_turned), (pick_sb, pick), (iota_sb, iota8), (power_sb, power)):
                sp.dma_start(dst[:], src).then_inc(consts_in, 16)
            slope_rows_in(0)
            slope_rows_in(1)
            parts_out(0)
            query_rows_in(0)
            query_rows_in(1)
            slope_rows_in(2)
            query_rows_in(2)
            parts_out(1)
            x_tile_in(2)
            for dst, src in ((wo_sb, wo), (gw_sb, gate_w), (gb_sb, gate_b.partition_broadcast(128))):
                sp.dma_start(dst[:, :], src).then_inc(wo_in, 16)
            negatives(0)
            slope_rows_in(3)
            query_rows_in(3)
            negatives(1)
            weights_in(0)
            for v in range(2, len(UNITS)):
                negatives(v)
                if v % NG == 1 and v // NG + 1 < NQT:
                    parts_out(v // NG + 1)
                if v + 2 < len(UNITS):
                    slope_rows_in(v + 2)
                    query_rows_in(v + 2)
                for e in range(NE):
                    if WEIGHTS_UNIT[e] == v:
                        weights_in(e)
                if v == NG:
                    experts_in()
                if v == 2 * NG - 1:
                    sp.wait_ge(side_free, TASK_NO["WO", 0] + 1)
                    x_tile_in(NQT - 1)
                for tt in range(NQT):
                    if STORE_UNIT[tt] == v:
                        store(tt)
            for tt in range(NQT):
                if STORE_UNIT[tt] == len(UNITS):
                    store(tt)
            sp.wait_ge(out_stored, 16 * NQT)

        @block.tensor
        def _(pe):
            mm = nc.tensor.matmul

            def chunk(ch):
                v, b, j, c = ch
                qt, g = UNITS[v]
                n = CHUNK_NO[ch]
                width = QT if c < qt else 128 * (b + 1)
                if n >= 2:
                    pe.wait_ge(chunks_maxed, n - 1)
                if ch == CHUNKS[v][0]:
                    pe.wait_ge(q_in[v % NQ], 64 * (v // NQ + 1))
                    if g == 0:
                        pe.wait_ge(k_in[qt], 32)
                mm(bank[:, MAX_BANK + n % 2, 0:width], q_rows[:, v % NQ, j, 128 * b:128 * (b + 1)],
                   k_rows[:, (G * g + j) // 2, c * QT:c * QT + width], start=True, stop=True).then_inc(max_full, 1)

            def scores(n):
                u, kb, j, skip, diagonal = slot_of(n)
                h = G * UNITS[u][1] + j
                if kb == 0 and j == 0:
                    pe.wait_ge(neg_in[u % 2], 32 * (u // 2 + 1))
                if n == FOUR_FROM:
                    pe.wait_ge(chunks_maxed, len(CHUNK_NO))
                if n >= 2:
                    ago = 4 if n >= FOUR_FROM + 4 else 2
                    pe.wait_ge(exp_done, n - ago + 1)
                last = mm(bank[:, score_bank(n), skip:QT], k_rows[:, h // 2, 128 * kb:128 * (kb + 1)],
                          q_rows[:, u % NQ, j, skip:QT], start=True, stop=not diagonal)
                if diagonal:
                    last = mm(bank[:, score_bank(n), skip:skip + 128], idh_sb[:, :], mask_t[:, :], start=False, stop=True)
                last.then_inc(scores_full, 1)

            def weighted(n):
                u, kb, j, skip, _ = slot_of(n)
                h = G * UNITS[u][1] + j
                if kb == 0 and u and j == 0:
                    pe.wait_ge(heads_t_done, u)
                pe.wait_ge(exp_done, n + 1)
                mm(bank[32 * j:32 * (j + 1), PV_BANK, skip:QT], v_sb[:, kb, VW * h:VW * h + 32],
                   weights[:, n % NW, skip:QT], start=kb == 0, stop=kb == KEYS[u] - 1).then_inc(pv_done, 1)

            def turn(src, dst=lambda b: side[:, 128 * b:128 * (b + 1)], idn=id_sb[:, :], n=NB):
                for b in range(n):
                    last = nc.tensor.transpose(dst(b), src(b), idn)
                return last

            def side_task(kind, n):
                no = TASK_NO[kind, n]
                if no:
                    pe.wait_ge(side_free, no)
                if kind == "XT":
                    pe.wait_ge(x_in[n], 16)
                    if n == 0:
                        pe.wait_ge(ident_in, 16)
                    last = turn(lambda b: x_sb[:, n % (NQT - 1), b, :])
                elif kind == "K":
                    if n == 0:
                        pe.wait_ge(wk_in, 16)
                    last = mm(side, wk_sb[:, :], xt_sb[:, :], start=True, stop=True)
                elif kind == "Q":
                    if n == 0:
                        pe.wait_ge(wq_in, 16)
                    last = mm(side, wq_sb[:, :], xt_sb[:, :], start=True, stop=True)
                elif kind == "V":
                    if n == 0:
                        pe.wait_ge(wv_in, 16)
                    for b in range(NB):
                        last = mm(side[:, 128 * b:128 * (b + 1)], xt_sb[:, 128 * b:128 * (b + 1)], wv_sb[:, :], start=True, stop=True)
                elif kind == "NEG":
                    pe.wait_ge(maxed, n + 1)
                    view = side[0:6, :].bitcast(bf16)
                    last = turn(lambda i: neg_parts[:, i % NB, i // NB, :, :].rearrange("p j t -> p (j t)"),
                                lambda i: view[:, 128 * i:128 * (i + 1)], idh_sb[:, :], NB * G // 2)
                elif kind == "HEADS":
                    pe.wait_ge(heads_t_done, n + 1)
                    last = turn(lambda b: heads_t[:, 128 * b:128 * (b + 1)])
                elif kind == "AT":
                    last = turn(lambda b: heads[:, b, :])
                elif kind == "WO":
                    pe.wait_ge(wo_in, 48)
                    for b in range(NB):
                        last = mm(side[:, 128 * b:128 * (b + 1)], attn_t[:, 128 * b:128 * (b + 1)], wo_sb[:, :], start=True, stop=True)
                elif kind == "X1T":
                    pe.wait_ge(x1_ready, n + 1)
                    last = turn(lambda b: x1[:, n % 2, b, :])
                elif kind == "GATE":
                    for b in range(NB):
                        last = mm(side[:, NE * b:NE * (b + 1)], x1_t[:, 128 * b:128 * (b + 1)], gw_sb[:, :], start=True, stop=True)
                elif kind == "CT":
                    pe.wait_ge(comb_ready, n + 1)
                    view = side[0:3 * NE, 0:QT // 2].bitcast(bf16)
                    last = turn(lambda b: comb_part[:, b, :, :].rearrange("p t e -> p (t e)"),
                                lambda b: view[:, 128 * b:128 * (b + 1)], idh_sb[:, :])
                elif kind == "COMB":
                    last = mm(side, pick_sb[:, n % NE, :], comb_th[:, n // NE % 2, :], start=True, stop=True)
                elif kind == "YT":
                    pe.wait_ge(y_added, (NE - 1) * (n + 1))
                    last = turn(lambda b: y_sum[:, 128 * b:128 * (b + 1)])
                last.then_inc(side_full, 1)

            def up(k, part):
                tt, e, fc = k // FSTEPS, k // FC % NE, k % FC
                w, x = ((w1_lo, x1_hi), (w1_hi, x1_lo), (w1_hi, x1_hi))[part]
                if part == 0:
                    if tt == 0 and fc == 0:
                        pe.wait_ge(w_split, 2 * e + 1)
                    if k % FSTEPS == 0:
                        pe.wait_ge(side_free, TASK_NO["X1T", tt] + 1)
                    if k == TWO_UPS_FROM + 1:
                        pe.wait_ge(exp_done, SLOTS)
                    elif k:
                        hid_wait(pe, k - 2 if k > TWO_UPS_FROM + 1 else k - 1)
                last = mm(bank[:, up_bank(k), :], w[:, e, 128 * fc:128 * (fc + 1)], x[:, tt % 2, :], start=part == 0, stop=part == 2)
                if part == 2:
                    last.then_inc(up_full, 1)

            def down(k, part):
                e, fc, m = k // FC % NE, k % FC, k // FC
                w, h = ((w2_lo, hid_hi), (w2_hi, hid_hi), (w2_hi, hid_lo))[part]
                if part == 0:
                    if k < FSTEPS and fc == 0:
                        pe.wait_ge(w_split, 2 * e + 2)
                    if m == TWO_YS_FROM + 1 and fc == 0:
                        pe.wait_ge(exp_done, SLOTS)
                    elif fc == 0 and m:
                        pe.wait_ge(y_weighed, m - 1 if m > TWO_YS_FROM + 1 else m)
                    hi_wait(pe, k)
                if part == 2:
                    lo_wait(pe, k)
                last = mm(bank[:, y_bank(m), :], w[:, e, 128 * fc:128 * (fc + 1)], h[:, k % 2, :],
                          start=fc == 0 and part == 0, stop=fc == FC - 1 and part == 2)
                if part == 2:
                    last.then_inc(down_done, 1)

            for tt in range(2):
                for kind in ("XT", "K", "Q", "V"):
                    side_task(kind, tt)
            pe.wait_ge(q_zero, 1)
            pe.wait_ge(key_rows_in, 32)
            pe.wait_ge(consts_in, 16 * 6)
            for ch in CHUNKS[0]:
                chunk(ch)
            for ch in CHUNKS_AHEAD[:4]:
                chunk(ch)
            side_task("NEG", 0)
            for ch in CHUNKS_AHEAD[4:]:
                chunk(ch)
            pe.wait_ge(v_ready, 1)
            for n in range(ALL_SLOTS):
                for m in [n] if n < FOUR_FROM else [n + 2] if n > FOUR_FROM else range(n, n + 3):
                    if m < SLOTS:
                        scores(m)
                for ch in CHUNKS_AT[n][:1]:
                    chunk(ch)
                if n % G == PV_LAG % G and 0 <= n - PV_LAG < SLOTS:
                    for j in range(G):
                        weighted(n - PV_LAG + j)
                for (kind, k), part in expert_parts(n):
                    (up if kind == "up" else down)(k, part)
                for ch in CHUNKS_AT[n][1:]:
                    chunk(ch)
                if SIDE[n]:
                    side_task(*SIDE[n])

        @block.scalar
        def _(act):
            copy, run = ACT.Copy, nc.scalar.activation

            def exps(n):
                skip = slot_of(n)[3]
                act.wait_ge(scores_full, n + 1)
                if n >= NW:
                    act.wait_ge(pv_done, n - NW + 1)
                run(weights[:, n % NW, skip:QT], bank[:, score_bank(n), skip:QT], ACT.Exp).then_inc(exp_done, 1)

            def sums_out(u):
                act.wait_ge(pv_done, UNIT_SLOT[u + 1])
                if u:
                    act.wait_ge(side_full, TASK_NO[("HEADS", u - 1) if u % NG else ("WO", u // NG - 1)] + 1)
                run(heads_t[:, :], bank[:, PV_BANK, :], copy).then_inc(heads_t_done, 1)

            def side_task(kind, n):
                if kind not in ("XT", "Q", "K", "AT", "X1T", "CT", "COMB"):
                    return
                act.wait_ge(side_full, TASK_NO[kind, n] + 1)
                if kind == "XT":
                    run(xt_sb[:, :], side, copy).then_inc(side_free, 1)
                elif kind == "Q":
                    if n:
                        act.wait_ge(q_split, n)
                    run(q32[:, :], side, copy, scale=float(HD) ** -0.5).then_inc(side_free, 1)
                elif kind == "K":
                    if n:
                        act.wait_ge(k_split, n)
                    run(k32[:, :], side, copy).then_inc(side_free, 1)
                elif kind == "AT":
                    run(attn_t[:, :], side, copy).then_inc(side_free, 1)
                elif kind == "X1T":
                    run(x1_t[:, :], side, copy)
                    run(x1_hi[:, n % 2, :], side, copy).then_inc(x1_hi_ready, 1)
                elif kind == "CT":
                    run(comb_th[:, n % 2, :], side[0:3 * NE, 0:QT // 2].bitcast(bf16), copy).then_inc(side_free, 1)
                elif kind == "COMB":
                    if n >= 2:
                        act.wait_ge(y_weighed, n - 1)
                    run(comb_b[:, n % 2, :], side, copy).then_inc(side_free, 1)

            def gap_exps(n):
                act.wait_ge(gap_ready, n + 1)
                run(gap_exp[:, :], gap[:, :], ACT.Exp).then_inc(gap_exp_ready, 1)

            def relus(k):
                e, fc = k // FC % NE, k % FC
                act.wait_ge(up_full, k + 1)
                if k == 0:
                    act.wait_ge(b1_in, 32)
                if k >= 2:
                    lo_wait(act, k - 2)
                run(hid[:, k % 2, :], bank[:, up_bank(k), :], ACT.Relu, bias=b1_sb[:, e, fc:fc + 1]).then_inc(hid_ready, 1)

            def high(k):
                hid_wait(act, k)
                if k >= 2:
                    act.wait_ge(down_done, k - 1)
                run(hid_hi[:, k % 2, :], hid[:, k % 2, :], copy).then_inc(hi_ready, 1)

            for task in AHEAD:
                side_task(*task)
            for n in range(ALL_SLOTS):
                if n < SLOTS:
                    exps(n)
                if n - PV_LAG + G in UNIT_SLOT[1:]:
                    sums_out(UNIT_SLOT.index(n - PV_LAG + G) - 1)
                for kind, k in EXPERTS_AT[n]:
                    if kind == "up" and not HID_BY_VECTOR[k]:
                        relus(k)
                for k in SPLIT_AT[n]:
                    if not HI_BY_VECTOR[k]:
                        high(k)
                if SIDE[n]:
                    side_task(*SIDE[n])
                if n >= 3 and SIDE[n - 3] and SIDE[n - 3][0] == "GATE":
                    gap_exps(SIDE[n - 3][1])

        @block.gpsimd
        def _(pool):
            count = [0]

            def link(ins):
                count[0] += 1
                ins.then_inc(pool_order, 1)
                pool.wait_ge(pool_order, count[0])

            def split_k(tt):
                pool.wait_ge(side_free, TASK_NO["K", tt] + 1)
                pool.wait_ge(k_out, 3 * 16 * tt)
                link(nc.gpsimd.tensor_copy(k_parts[:, 0, :], k32[:, :]))
                link(nc.gpsimd.tensor_tensor(k32[:, :], k32[:, :], k_parts[:, 0, :], ALU.subtract))
                link(nc.gpsimd.tensor_copy(k_parts[:, 1, :], k32[:, :]))
                nc.gpsimd.tensor_tensor(k_parts[:, 2, :], k32[:, :], k_parts[:, 1, :], ALU.subtract).then_inc(k_split, 1)

            def split_w(e):
                for i, (hi, lo) in enumerate(((w1_hi, w1_lo), (w2_hi, w2_lo))):
                    pool.wait_ge(w_in[i], 16 * (e + 1))
                    link(nc.gpsimd.tensor_copy(hi[:, e, :], w_raw[:, i, :]))
                    nc.gpsimd.tensor_tensor(lo[:, e, :], w_raw[:, i, :], hi[:, e, :].bitcast(f32), ALU.subtract).then_inc(w_split, 1)

            def low(k):
                hi_wait(pool, k)
                nc.gpsimd.tensor_tensor(hid_lo[:, k % 2, :], hid[:, k % 2, :], hid_hi[:, k % 2, :].bitcast(f32), ALU.subtract).then_inc(lo_ready, 1)

            def rstds(n):
                pool.wait_ge(var_ready, n + 1)
                nc.gpsimd.tensor_tensor(rstd[:, :], var_eps[:, :], power_sb[:, :], ALU.pow).then_inc(rstd_ready, 1)

            def add_y(m):
                pool.wait_ge(y_weighed, m + 1)
                nc.gpsimd.tensor_tensor(y_sum[:, :], y_sum[:, :], y_part[:, m % 2, :], ALU.add).then_inc(y_added, 1)
                pool.wait_ge(y_added, m + 1 - (m + NE) // NE)

            link(nc.gpsimd.memset(v_sb[:, :, :], 0.0))
            nc.gpsimd.memset(v_heads[:, :, :, HD:HD + 1], 1.0).then_inc(v_ready, 1)
            pool.wait_ge(consts_in, 16 * 6)
            split_k(1)
            for n in range(ALL_SLOTS):
                for e in range(NE):
                    if SPLIT_SLOT[e] == n:
                        split_w(e)
                for k in SPLIT_AT[n]:
                    if not LO_BY_VECTOR[k]:
                        low(k)
                if SIDE[n]:
                    kind, k = SIDE[n]
                    if kind == "K":
                        split_k(k)
                    if kind in ("WO", "YT"):
                        rstds(LN_NO[kind, k])
                for kind, k in EXPERTS_AT[n]:
                    if kind == "down" and k % FC == FC - 1 and k // FC % NE and k < NQT * FSTEPS - 1:
                        add_y(k // FC)

        @block.vector
        def _(dve):
            v_ = nc.vector
            count = [0]

            def link(ins):
                count[0] += 1
                ins.then_inc(vec_order, 1)
                dve.wait_ge(vec_order, count[0])

            def maxes(ch):
                v, b, j, c = ch
                n = CHUNK_NO[ch]
                dve.wait_ge(max_full, n + 1)
                to = chunk_max[:, v % 2, b * G + j, c:c + 1]
                if c < UNITS[v][0]:
                    v_.tensor_reduce(to, bank[:, MAX_BANK + n % 2, :], axis=AX.X, op=ALU.max).then_inc(chunks_maxed, 1)
                else:
                    w = 128 * (b + 1)
                    v_.tensor_tensor_reduce(out=bank[:, MAX_BANK + n % 2, 0:w], in0=bank[:, MAX_BANK + n % 2, 0:w], in1=mask_sb[:, QT - w:QT],
                                            scale=1.0, scalar=MASKED, op0=ALU.add, op1=ALU.max, accum_out=to).then_inc(chunks_maxed, 1)

            def unit_max(v):
                qt, g = UNITS[v]
                dve.wait_ge(chunks_maxed, CHUNK_NO[CHUNKS[v][-1]] + 1)
                if v:
                    dve.wait_ge(side_full, TASK_NO["NEG", v - 1] + 1)
                link(v_.tensor_reduce(row_max[:, :], chunk_max[:, v % 2, :, 0:qt + 1], axis=AX.X, op=ALU.max))
                parts = neg_parts[:, :, :, :, :].rearrange("p b i j t -> p (b i j) t")
                link(v_.tensor_scalar(parts[:, :, 0], row_max[:, :], -1.0, None, ALU.mult))
                link(v_.scalar_tensor_tensor(out=max_rest[:, :], in0=row_max[:, :], scalar=-1.0, in1=parts[:, :, 0],
                                             op0=ALU.mult, op1=ALU.subtract))
                link(v_.tensor_copy(parts[:, :, 1], max_rest[:, :]))
                v_.tensor_tensor(parts[:, :, 2], max_rest[:, :], parts[:, :, 1], ALU.subtract).then_inc(maxed, 1)

            def ln_stats(src, stat, mv):
                for b in range(NB):
                    last = v_.bn_stats(stat[:, b, :], src[:, b, :])
                link(last)
                for b in range(NB):
                    last = v_.bn_aggr(mv[:, b, :], stat[:, b, :])
                link(last)
                v_.tensor_scalar(var_eps[:, :], mv[:, :, 1], EPS, None, ALU.add).then_inc(var_ready, 1)

            def ln_apply(src, mv, dst, n, done):
                dve.wait_ge(rstd_ready, n + 1)
                for b in range(NB):
                    last = v_.tensor_scalar(dst[:, b, :], src[:, b, :], mv[:, b, 0:1], rstd[:, b:b + 1], ALU.subtract, ALU.mult)
                last.then_inc(done, 1)

            def split(rest, parts, done):
                link(v_.tensor_copy(parts[:, 0, :], rest[:, :]))
                link(v_.tensor_tensor(rest[:, :], rest[:, :], parts[:, 0, :], ALU.subtract))
                link(v_.tensor_copy(parts[:, 1, :], rest[:, :]))
                v_.tensor_tensor(parts[:, 2, :], rest[:, :], parts[:, 1, :], ALU.subtract).then_inc(done, 1)

            def side_task(kind, n):
                if kind == "Q":
                    dve.wait_ge(side_free, TASK_NO["Q", n] + 1)
                    if n:
                        dve.wait_ge(q_out, 3 * 16 * n)
                    split(q32, q_parts, q_split)
                if kind == "K" and n == 0:
                    dve.wait_ge(side_free, TASK_NO["K", 0] + 1)
                    split(k32, k_parts, k_split)
                if kind not in ("V", "NEG", "HEADS", "WO", "X1T", "GATE", "YT"):
                    return
                dve.wait_ge(side_full, TASK_NO[kind, n] + 1)
                if kind == "V":
                    if n == 0:
                        dve.wait_ge(v_ready, 1)
                    v_.tensor_copy(v_heads[:, NB * n:NB * (n + 1), :, 0:HD],
                                   side.rearrange("p (b h d) -> p b h d", b=NB, h=NH)).then_inc(side_free, 1)
                elif kind == "NEG":
                    if n >= 2:
                        dve.wait_ge(neg_in[n % 2], 32 * (n // 2))
                    v_.tensor_copy(neg_rows[:, n % 2, :, :], side[0:6, :].bitcast(bf16).rearrange("p (i c) -> p i c", i=G // 2)).then_inc(neg_ready, 1)
                    dve.wait_ge(neg_ready, n + 1)
                    v_.sem_inc(side_free, 1)
                elif kind == "HEADS":
                    qt, g = UNITS[n]
                    sums = side.rearrange("p (b j r) -> p b j r", b=NB, j=G)
                    link(v_.reciprocal(inv_sum[:, :, :], sums[:, :, :, HD]))
                    v_.tensor_tensor(heads[:, :, 32 * g:32 * (g + 1)].rearrange("p b (j d) -> p b j d", j=G), sums[:, :, :, 0:HD],
                                     inv_sum[:, :, :].unsqueeze(3).to_broadcast([128, NB, G, HD]), ALU.mult).then_inc(side_free, 1)
                elif kind == "WO":
                    v_.tensor_tensor(pre[:, :, :], side.rearrange("p (b c) -> p b c", b=NB), x_sb[:, n % (NQT - 1), :, :],
                                     ALU.add).then_inc(side_free, 1)
                    dve.wait_ge(side_free, TASK_NO[kind, n] + 1)
                    ln_stats(pre, stats, mean_var)
                elif kind == "X1T":
                    dve.wait_ge(x1_hi_ready, n + 1)
                    v_.tensor_tensor(x1_lo[:, n % 2, :], side, x1_hi[:, n % 2, :].bitcast(f32), ALU.subtract).then_inc(side_free, 1)
                elif kind == "GATE":
                    v_.tensor_tensor(score[:, :, :], side[:, 0:NB * NE].rearrange("p (b e) -> p b e", b=NB),
                                     gb_sb[:, :].unsqueeze(1).to_broadcast([128, NB, NE]), ALU.add).then_inc(side_free, 1)
                    dve.wait_ge(side_free, TASK_NO[kind, n] + 1)
                    for b in range(NB):
                        last = v_.max(top[:, b, :], score[:, b, :])
                    link(last)
                    v_.tensor_tensor(gap[:, :], top[:, :, 1], top[:, :, 0], ALU.subtract).then_inc(gap_ready, 1)
                    for b in range(NB):
                        last = v_.max_index(top_at[:, b, :], top[:, b, :], score[:, b, :])
                    link(last)
                    link(v_.tensor_copy(top_atf[:, :, :], top_at[:, :, :]))
                elif kind == "YT":
                    v_.tensor_tensor(pre[:, :, :], side.rearrange("p (b c) -> p b c", b=NB), x1[:, n % 2, :, :],
                                     ALU.add).then_inc(side_free, 1)
                    dve.wait_ge(side_free, TASK_NO[kind, n] + 1)
                    ln_stats(pre, stats, mean_var)

            def combine(n):
                dve.wait_ge(gap_exp_ready, n + 1)
                link(v_.tensor_scalar(prob[:, 2, :], gap_exp[:, :], 1.0, None, ALU.add))
                link(v_.reciprocal(prob[:, 0, :], prob[:, 2, :]))
                link(v_.tensor_tensor(prob[:, 1, :], prob[:, 0, :], gap_exp[:, :], ALU.mult))
                for b in range(NB):
                    v_.tensor_scalar(first[:, b, :], iota_sb[:, :], top_atf[:, b, 0:1], prob[:, 0, b:b + 1], ALU.is_equal, ALU.mult)
                    last = v_.tensor_scalar(second[:, b, :], iota_sb[:, :], top_atf[:, b, 1:2], prob[:, 1, b:b + 1], ALU.is_equal, ALU.mult)
                link(last)
                link(v_.tensor_tensor(comb[:, :, :], first[:, :, :], second[:, :, :], ALU.add))
                link(v_.tensor_copy(comb_part[:, :, 0, :], comb[:, :, :]))
                link(v_.tensor_tensor(comb_rest[:, :, :], comb[:, :, :], comb_part[:, :, 0, :], ALU.subtract))
                link(v_.tensor_copy(comb_part[:, :, 1, :], comb_rest[:, :, :]))
                v_.tensor_tensor(comb_part[:, :, 2, :], comb_rest[:, :, :], comb_part[:, :, 1, :], ALU.subtract).then_inc(comb_ready, 1)

            def relus(k):
                e, fc = k // FC % NE, k % FC
                dve.wait_ge(up_full, k + 1)
                if k >= 2:
                    lo_wait(dve, k - 2)
                v_.tensor_scalar(hid[:, k % 2, :], bank[:, up_bank(k), :], b1_sb[:, e, fc:fc + 1], 0.0, ALU.add, ALU.max).then_inc(hid_ready_v, 1)

            def low(k):
                hi_wait(dve, k)
                v_.tensor_tensor(hid_lo[:, k % 2, :], hid[:, k % 2, :], hid_hi[:, k % 2, :].bitcast(f32), ALU.subtract).then_inc(lo_ready_v, 1)

            def weigh_y(m):
                tt, e = m // NE, m % NE
                dve.wait_ge(down_done, FC * (m + 1))
                dve.wait_ge(side_free, TASK_NO["COMB", m] + 1)
                if m == 0:
                    dve.wait_ge(b1_in, 32)
                if e == 0:
                    if tt:
                        dve.wait_ge(side_full, TASK_NO["YT", tt - 1] + 1)
                    to = y_sum[:, :]
                else:
                    if m >= 3:
                        before = m - 2 if (m - 2) % NE else m - 3
                        dve.wait_ge(y_added, before - before // NE)
                    to = y_part[:, m % 2, :]
                v_.scalar_tensor_tensor(out=to, in0=bank[:, y_bank(m), :], scalar=b2_sb[:, e:e + 1], in1=comb_b[:, m % 2, :],
                                        op0=ALU.add, op1=ALU.mult).then_inc(y_weighed, 1)
                if m == NQT * NE - 1:
                    dve.wait_ge(y_weighed, m + 1)
                    dve.wait_ge(y_added, (NE - 1) * NQT - 1)
                    v_.tensor_tensor(y_sum[:, :], y_sum[:, :], y_part[:, m % 2, :], ALU.add).then_inc(y_added, 1)

            v_.memset(q_rows[HROWS:128, :, 0::2, :].bitcast(u32), 0)
            v_.memset(q_rows[0:HROWS, :, 1::2, :].bitcast(u32), 0).then_inc(q_zero, 1)
            for kind, tt in (("K", 0), ("Q", 0), ("V", 0), ("Q", 1), ("V", 1)):
                side_task(kind, tt)
            dve.wait_ge(consts_in, 16 * 6)
            for ch in CHUNKS[0]:
                maxes(ch)
            unit_max(0)
            for ch in CHUNKS_AHEAD[:2]:
                maxes(ch)
            side_task("NEG", 0)
            for ch in CHUNKS_AHEAD[2:]:
                maxes(ch)
            dve.wait_ge(wo_in, 48)
            for n in range(ALL_SLOTS):
                for ch in CHUNKS_AT[n]:
                    maxes(ch)
                if n in MAXED_AFTER:
                    unit_max(MAXED_AFTER[n])
                for kind, k in EXPERTS_AT[n]:
                    if kind == "up" and HID_BY_VECTOR[k]:
                        relus(k)
                    if kind == "down" and k % FC == FC - 1:
                        weigh_y(k // FC)
                for k in SPLIT_AT[n]:
                    if HI_BY_VECTOR[k]:
                        hid_wait(dve, k)
                        if k >= 2:
                            dve.wait_ge(down_done, k - 1)
                        v_.tensor_copy(hid_hi[:, k % 2, :], hid[:, k % 2, :]).then_inc(hi_ready_v, 1)
                    if LO_BY_VECTOR[k]:
                        low(k)
                if SIDE[n]:
                    side_task(*SIDE[n])
                late = SIDE.get(n - 6)
                if late and late[0] == "WO":
                    ln_apply(pre, mean_var, x1[:, late[1] % 2, :, :], LN_NO[late], x1_ready)
                if late and late[0] == "YT":
                    if late[1] == 0:
                        dve.wait_ge(k_split, NQT)
                    if late[1]:
                        dve.wait_ge(out_stored, 16 * late[1])
                    ln_apply(pre, mean_var, out_sb, LN_NO[late], out_ready)
                late = SIDE.get(n - 5)
                if late and late[0] == "GATE":
                    combine(late[1])


def shape_constants():
    import numpy as np
    half = np.dtype("bfloat16")
    start = 2.0 ** (-2.0 ** (3 - NH.bit_length() + 1))
    slopes = np.array([start * start ** h for h in range(NH)], np.float64).astype(np.float32)
    s1 = slopes.astype(half)
    s2 = (slopes - s1.astype(np.float32)).astype(half)
    s3 = (slopes - s1.astype(np.float32) - s2.astype(np.float32)).astype(half)
    parts = np.stack([s1, s2, s3]).astype(np.float32)
    key_rows = np.zeros((CR, T), np.float32)
    key_rows[0:3] = np.arange(T) % 128
    key_rows[3:6] = np.arange(T) // 128
    key_rows[NEG_ROW:NEG_ROW + 3] = 1
    query_rows = np.zeros((CR, NH, QT), np.float32)
    query_rows[0:3] = parts[:, :, None]
    query_rows[3:6] = 128 * parts[:, :, None]
    mask = np.zeros((128, QT), np.float32)
    mask[:, QT - 128:] = np.where(np.arange(128)[None, :] > np.arange(128)[:, None], np.float32(MASKED), np.float32(0))
    pick = np.zeros((3 * NE, NE, 128), np.float32)
    for e in range(NE):
        for t in range(3):
            pick[t * NE + e, e, :] = 1
    return {
        "ident": np.eye(128, dtype=np.float32), "ident_h": np.eye(128).astype(half),
        "key_rows": key_rows.astype(half), "query_rows": query_rows.astype(half), "mask": mask.astype(half), "mask_turned": mask[:, QT - 128:].T.astype(half), "pick": pick.astype(half),
        "iota8": np.tile(np.arange(NE, dtype=np.float32), (128, 1)), "power": np.full((128, NB), -0.5, np.float32),
    }


_INS = ["L0_attn_x", "L0_attn_Wq", "L0_attn_Wk", "L0_attn_Wv", "L0_attn_Wo", "L0_ffn_gate_w", "L0_ffn_gate_b",
        "L0_ffn_W1", "L0_ffn_b1", "L0_ffn_W2", "L0_ffn_b2"]


def kernel(**inputs):
    import numpy as _np
    import concourse.bacc as _bacc
    from concourse import mybir as _mybir
    from concourse.bass_utils import run_bass_kernel_spmd as _run

    nc = _bacc.Bacc("TRN2", target_bir_lowering=False, num_devices=1)
    arrays, args = {}, []
    given = {name: _np.ascontiguousarray(inputs[name]) for name in _INS}
    b1 = given["L0_ffn_b1"].reshape(NE, FC, 128)
    given["L0_ffn_b1"] = _np.ascontiguousarray(b1.transpose(2, 0, 1))
    given["L0_ffn_b2"] = _np.ascontiguousarray(given["L0_ffn_b2"].T)
    for name, a in {**given, **shape_constants()}.items():
        arrays[f"in_{name}"] = a
        args.append(nc.dram_tensor(f"in_{name}", a.shape, _mybir.dt.from_np(a.dtype), kind="ExternalInput").ap())
    args.append(nc.dram_tensor("out_0", (1, T, C), _mybir.dt.float32, kind="ExternalOutput").ap())
    layer_kernel(nc, *args)
    r = _run(nc, [arrays], core_ids=[0])
    return r.results[0]["out_0"]
```
